# Optimizing a Trainium2 kernel written in Bass

```python
import numpy as np
import jax
import jax.numpy as jnp

def _softmax(x, axis=-1):
    return jax.nn.softmax(x, axis=axis)

def _gelu(x):
    return jax.nn.gelu(x, approximate=True)

def _silu(x):
    return jax.nn.silu(x)

def _sigmoid(x):
    return jax.nn.sigmoid(x)

def _layernorm(x, axis=-1, eps=1e-05):
    m = jnp.mean(x, axis=axis, keepdims=True)
    v = jnp.var(x, axis=axis, keepdims=True)
    return (x - m) / jnp.sqrt(v + eps)

def _scatter_add(tgt, idx, src, axis=0):
    return tgt.at[idx].add(src)

def _segment_sum(src, seg, n):
    return jax.ops.segment_sum(src, seg, n)
kernel_name = 'mk_conv_attn_hybrid_d2_conv_nhwc128_r2_903b48'

def setup_inputs(seed: int=0):
    np.random.seed(seed)
    _w = jnp.asarray

    def _rec_inputs():
        import jax
        import jax.numpy as jnp
        _gk = jax.random.key(seed)
        x = 7.22e-05 + 1 * jax.random.normal(jax.random.fold_in(_gk, 1), (16, 32, 32, 64), jnp.float32)
        return x
    x = _rec_inputs()

    def _L0_conv_setup():
        import jax, jax.numpy as jnp
        import numpy as np
        EPS = 1e-06

        def group_norm(x, scale, bias, num_groups):
            B, H, W, C = x.shape
            xg = x.reshape(B, H, W, num_groups, C // num_groups)
            mean = jnp.mean(xg, axis=(1, 2, 4), keepdims=True)
            var = jnp.var(xg, axis=(1, 2, 4), keepdims=True)
            xg = (xg - mean) * jax.lax.rsqrt(var + EPS)
            return xg.reshape(B, H, W, C) * scale + bias

        def nin(h, w, b):
            return jnp.einsum('bhwc,cd->bhwd', h, w) + b
        key = jax.random.key(seed)
        ks = jax.random.split(key, 8)
        B, H, W, C = (16, 32, 32, 64)
        s = 1.0 / np.sqrt(C)
        return {'x': jax.random.normal(ks[0], (B, H, W, C), jnp.float32), 'gn_scale': jnp.ones((C,), jnp.float32), 'gn_bias': jnp.zeros((C,), jnp.float32), 'wq': jax.random.normal(ks[1], (C, C), jnp.float32) * s, 'bq': jnp.zeros((C,), jnp.float32), 'wk': jax.random.normal(ks[2], (C, C), jnp.float32) * s, 'bk': jnp.zeros((C,), jnp.float32), 'wv': jax.random.normal(ks[3], (C, C), jnp.float32) * s, 'bv': jnp.zeros((C,), jnp.float32), 'wo': jax.random.normal(ks[4], (C, C), jnp.float32) * s, 'bo': jnp.zeros((C,), jnp.float32)}
    _L0_conv_all = _L0_conv_setup()
    _L0_conv_in = {k: v for k, v in _L0_conv_all.items() if k in ('gn_scale', 'gn_bias', 'wq', 'bq', 'wk', 'bk', 'wv', 'bv', 'wo', 'bo')}
    del _L0_conv_all

    def _L1_attn_setup():
        import jax, jax.numpy as jnp
        import numpy as np
        B, S, D = (4, 2048, 64)
        key = jax.random.key(seed)
        kx, kq, kk, kv = jax.random.split(key, 4)
        x = jax.random.normal(kx, (B, S, D), dtype=jnp.float32)
        Wq = jax.random.normal(kq, (D, D), dtype=jnp.float32) * (1.0 / np.sqrt(D))
        Wk = jax.random.normal(kk, (D, D), dtype=jnp.float32) * (1.0 / np.sqrt(D))
        Wv = jax.random.normal(kv, (D, D), dtype=jnp.float32) * (1.0 / np.sqrt(D))
        return {'x': x, 'Wq': Wq, 'Wk': Wk, 'Wv': Wv}
    _L1_attn_all = _L1_attn_setup()
    _L1_attn_in = {k: v for k, v in _L1_attn_all.items() if k in ('Wq', 'Wk', 'Wv')}
    del _L1_attn_all

    def _L1_ffn_setup():
        import jax, jax.numpy as jnp
        import numpy as np
        B, S, D, E, H, O, K = (256, 1024, 64, 32, 256, 64, 8)
        key = jax.random.key(seed)
        k0, k1, k2, k3 = jax.random.split(key, 4)
        x = jax.random.normal(k0, (B, S, D), dtype=jnp.float32)
        gate_w = jax.random.normal(k1, (E, D), dtype=jnp.float32) * (1.0 / np.sqrt(D))
        gate_b = jnp.zeros((E,), dtype=jnp.float32)
        weight1 = jax.random.uniform(k2, (E, D + 1, H), dtype=jnp.float32, minval=-1.0, maxval=1.0) * (1.0 / np.sqrt(D + 1))
        weight2 = jax.random.uniform(k3, (E, H + 1, O), dtype=jnp.float32, minval=-1.0, maxval=1.0) * (1.0 / np.sqrt(H + 1))
        return {'x': x, 'gate_w': gate_w, 'gate_b': gate_b, 'weight1': weight1, 'weight2': weight2}
    _L1_ffn_all = _L1_ffn_setup()
    _L1_ffn_in = {k: v for k, v in _L1_ffn_all.items() if k in ('gate_w', 'gate_b', 'weight1', 'weight2')}
    del _L1_ffn_all
    return {'x': x, 'L0_conv_gn_scale': _L0_conv_in['gn_scale'], 'L0_conv_gn_bias': _L0_conv_in['gn_bias'], 'L0_conv_wq': _L0_conv_in['wq'], 'L0_conv_bq': _L0_conv_in['bq'], 'L0_conv_wk': _L0_conv_in['wk'], 'L0_conv_bk': _L0_conv_in['bk'], 'L0_conv_wv': _L0_conv_in['wv'], 'L0_conv_bv': _L0_conv_in['bv'], 'L0_conv_wo': _L0_conv_in['wo'], 'L0_conv_bo': _L0_conv_in['bo'], 'L1_attn_Wq': _L1_attn_in['Wq'], 'L1_attn_Wk': _L1_attn_in['Wk'], 'L1_attn_Wv': _L1_attn_in['Wv'], 'L1_ffn_gate_w': _L1_ffn_in['gate_w'], 'L1_ffn_gate_b': _L1_ffn_in['gate_b'], 'L1_ffn_weight1': _L1_ffn_in['weight1'], 'L1_ffn_weight2': _L1_ffn_in['weight2']}

def reference(x, L0_conv_gn_scale, L0_conv_gn_bias, L0_conv_wq, L0_conv_bq, L0_conv_wk, L0_conv_bk, L0_conv_wv, L0_conv_bv, L0_conv_wo, L0_conv_bo, L1_attn_Wq, L1_attn_Wk, L1_attn_Wv, L1_ffn_gate_w, L1_ffn_gate_b, L1_ffn_weight1, L1_ffn_weight2):
    import jax
    import jax.numpy as jnp

    def _L0_conv_ref(x, gn_scale, gn_bias, wq, bq, wk, bk, wv, bv, wo, bo):
        import jax, jax.numpy as jnp
        import numpy as np
        EPS = 1e-06

        def group_norm(x, scale, bias, num_groups):
            B, H, W, C = x.shape
            xg = x.reshape(B, H, W, num_groups, C // num_groups)
            mean = jnp.mean(xg, axis=(1, 2, 4), keepdims=True)
            var = jnp.var(xg, axis=(1, 2, 4), keepdims=True)
            xg = (xg - mean) * jax.lax.rsqrt(var + EPS)
            return xg.reshape(B, H, W, C) * scale + bias

        def nin(h, w, b):
            return jnp.einsum('bhwc,cd->bhwd', h, w) + b
        B, H, W, C = x.shape
        num_groups = min(C // 4, 32)
        h = group_norm(x, gn_scale, gn_bias, num_groups)
        q = nin(h, wq, bq)
        k = nin(h, wk, bk)
        v = nin(h, wv, bv)
        w = jnp.einsum('bhwc,bHWc->bhwHW', q, k) * C ** (-0.5)
        w = w.reshape(B, H, W, H * W)
        w = jax.nn.softmax(w, axis=-1)
        w = w.reshape(B, H, W, H, W)
        h = jnp.einsum('bhwHW,bHWc->bhwc', w, v)
        h = nin(h, wo, bo)
        return x + h

    def _L1_attn_ref(x, Wq, Wk, Wv):
        import jax, jax.numpy as jnp
        import numpy as np
        B, S, D = (4, 2048, 64)
        b, s, d = x.shape
        q = jnp.einsum('bsd,ed->bse', x, Wq)
        k = jnp.einsum('bsd,ed->bse', x, Wk)
        v = jnp.einsum('bsd,ed->bse', x, Wv)
        scores = jnp.einsum('bqd,bkd->bqk', q, k) / jnp.sqrt(jnp.float32(d))
        causal = jnp.tril(jnp.ones((s, s), dtype=bool))
        scores = jnp.where(causal, scores, jnp.float32(-jnp.inf))
        weights = jax.nn.softmax(scores.astype(jnp.float32), axis=-1)
        out = jnp.einsum('bqk,bkd->bqd', weights, v)
        return out

    def _L1_ffn_ref(x, gate_w, gate_b, weight1, weight2):
        import jax, jax.numpy as jnp
        import numpy as np
        B, S, D, E, H, O, K = (256, 1024, 64, 32, 256, 64, 8)
        Bn, Sn, Dn = x.shape
        logits = jnp.einsum('bsd,ed->bse', x, gate_w) + gate_b
        probs = jax.nn.softmax(logits, axis=1)
        vals, idx = jax.lax.top_k(probs.transpose(0, 2, 1), K)
        topv = vals.transpose(0, 2, 1)
        topi = idx.transpose(0, 2, 1)
        flat_idx = topi.reshape(Bn, K * E)
        gathered = jnp.take_along_axis(x, flat_idx[:, :, None], axis=1)
        gathered = gathered.reshape(Bn, K, E, Dn)
        pooled = jnp.einsum('bked,bke->bed', gathered, topv)
        ones = jnp.ones((E, Bn, 1), dtype=x.dtype)
        h = jnp.concatenate([pooled.transpose(1, 0, 2), ones], axis=-1)
        h = jax.nn.gelu(jnp.einsum('ebd,edh->ebh', h, weight1), approximate=False)
        h = jnp.concatenate([h, ones], axis=-1)
        out = jnp.einsum('ebh,eho->ebo', h, weight2)
        out = out.transpose(1, 0, 2)
        weighted = jnp.einsum('beo,bke->bkeo', out, topv).reshape(Bn, K * E, O)
        outputs = jnp.zeros((Bn, Sn, O), dtype=x.dtype)
        outputs = outputs.at[jnp.arange(Bn)[:, None], flat_idx].add(weighted)
        return outputs

    def _gn(v, G=32, eps=1e-05):
        B_, H_, W_, C_ = v.shape
        g = v.reshape(B_, H_, W_, G, C_ // G)
        m = jnp.mean(g, axis=(1, 2, 4), keepdims=True)
        s = jnp.var(g, axis=(1, 2, 4), keepdims=True)
        return ((g - m) / jnp.sqrt(s + eps)).reshape(v.shape)

    def _ln_c(v, eps=1e-06):
        m = jnp.mean(v, axis=-1, keepdims=True)
        s = jnp.var(v, axis=-1, keepdims=True)
        return (v - m) / jnp.sqrt(s + eps)

    def _ln_t(v, eps=1e-05):
        m = jnp.mean(v, axis=-1, keepdims=True)
        s = jnp.var(v, axis=-1, keepdims=True)
        return (v - m) / jnp.sqrt(s + eps)

    def _to_tokens(v):
        B_, H_, W_, C_ = v.shape
        return v.reshape(B_, H_ * W_, C_)

    def _from_tokens(t, like):
        return t.reshape(like.shape)
    x = _L0_conv_ref(x, L0_conv_gn_scale, L0_conv_gn_bias, L0_conv_wq, L0_conv_bq, L0_conv_wk, L0_conv_bk, L0_conv_wv, L0_conv_bv, L0_conv_wo, L0_conv_bo)
    t = _to_tokens(x)
    t = t + _L1_attn_ref(_ln_t(t), L1_attn_Wq, L1_attn_Wk, L1_attn_Wv)
    t = t + _L1_ffn_ref(_ln_t(t), L1_ffn_gate_w, L1_ffn_gate_b, L1_ffn_weight1, L1_ffn_weight2)
    x = _from_tokens(t, x)
    return x

_drawn_inputs = setup_inputs


def setup_inputs(seed=0):
    import zlib

    import numpy as np

    out = dict(_drawn_inputs(seed))
    spreads = {'L0_conv_gn_scale': (1.0, 0.2),
     'L0_conv_gn_bias': (0.0, 0.1),
     'L0_conv_bq': (0.0, 0.459),
     'L0_conv_bk': (0.0, 0.8),
     'L0_conv_bv': (0.0, 0.1),
     'L0_conv_bo': (0.0, 0.1),
     'L1_ffn_gate_b': (0.0, 0.8)}
    factors = {'L1_ffn_gate_w': 8.0, 'L1_ffn_weight1': 8.0, 'L1_ffn_weight2': 8.0}
    for name, (base, spread) in spreads.items():
        noise = np.random.default_rng([zlib.crc32(name.encode()), seed]).standard_normal(out[name].shape)
        drawn = base * np.exp(spread * noise) if base else spread * noise
        out[name] = jnp.asarray(drawn.astype(out[name].dtype))
    for name, factor in factors.items():
        out[name] = (out[name] * factor).astype(out[name].dtype)
    return out
```

```python
from contextlib import ExitStack

import numpy as np

import concourse.bass as bass
from concourse import mybir

ALU = mybir.AluOpType
ACT = mybir.ActivationFunctionType
AX = mybir.AxisListType
F32 = mybir.dt.float32
F32R = mybir.dt.float32r
BF16 = mybir.dt.bfloat16

B, S, C = 16, 1024, 64
P = 128
NT = S // P
NJ = NT // 2
HALF = S // 2
E, HID, TOPK = 32, 256, 8
GROUP = 4
SCALE = float(C) ** -0.5
EPS_GN, EPS_LN = 1e-6, 1e-5
MASKED = -1e30
KROWS = C + NT
NEG_HUGE = -3e38
NST, NP = 3, 4
BG = 4

UNITS_1 = [(t, a, 0) for t in range(NT) for a in range(2)]
UNITS_2 = [(t, a, j0) for t in range(NT) for a, j0 in ((0, (t + 1) // 2), (1, t // 2)) if j0 < NJ]
UNITS = {1: UNITS_1, 2: UNITS_2}
PIECES_1 = [(c, h, NJ) for c in range(NT) for h in range(2)]
PIECES_2 = [(c, h, w) for c in range(NT)
            for h, w in ((0, (2 * (c % NJ) + c // NJ) // 2 + 1), (1, (2 * (c % NJ) + c // NJ + 1) // 2)) if w]
PIECES = {1: PIECES_1, 2: PIECES_2}

SIDES_1 = {0: [("p1.tr", 1)], 2: [("p1.g1", 1)], 3: [("f2.rs", -2)], 4: [("p1.g2", 1)],
           5: [("p1.h", 1)], 6: [("f2.out", -2), ("l2", -2)], 8: [("p1.qa", 1)], 9: [("p1.qb", 1)],
           10: [("p1.ka", 1)], 11: [("moe.tr", -2)], 12: [("p1.kb", 1)], 13: [("moe.lg", -2)],
           15: [("r2", -1)]}
SIDES_2 = {3: [("f1.rs", 0)], 6: [("f1.out", 0), ("l1", 0)], 10: [("p2.tr", 0)],
           12: [("p2.qa", 0)], 14: [("p2.qb", 0), ("r1", 1)]}
SIDES = {1: SIDES_1, 2: SIDES_2}
PIECE_SLOTS = {1: [p * 13 // 16 for p in range(len(PIECES_2))], 2: [p * 13 // 16 for p in range(len(PIECES_1))]}
STEPS = {
    "p1.tr": ["tr", "xt", "bn", "ag"], "p1.g1": ["mm", "gv", "d", "d2"],
    "p1.g2": ["mm", "ve", "rstd", "a", "ma", "b"], "p1.h": ["hf", "hh", "la", "lb", "hi"],
    "p1.qa": ["mm", "hi", "lo"], "p1.qb": ["mm", "hi", "lo"], "p1.ka": ["mm", "hi", "lo"],
    "p1.kb": ["mm", "hi", "lo", "k2"],
    "p2.tr": ["tr", "hh", "hi", "lo"], "p2.qa": ["mm", "hi", "lo"], "p2.qb": ["mm", "hi", "lo", "k2"],
    "f1.rs": ["mm", "ri", "on", "aff"], "f1.out": ["mm", "t"],
    "f2.rs": ["mm", "ri", "on"], "f2.out": ["mm", "t"],
    "moe.tr": ["tr", "ut"], "moe.lg": ["mm", "lg"],
    "r1": ["neg", "tr", "row"], "r2": ["neg", "tr", "row"],
    "l1": ["sum", "nm", "xc", "sq", "vs", "ve", "rs", "v"],
    "l2": ["sum", "nm", "xc", "sq", "vs", "ve", "rs", "v"],
}
CHAIN = {"p1": "proj_step", "p2": "proj_step", "f1": "fin_step", "f2": "fin_step", "mo": "fin_step",
         "r1": "fin_step", "r2": "fin_step", "l1": "norm_step", "l2": "norm_step"}
LOOP_FIRST, LOOP_TRIPS = 2, 6
LAST = B


def main_runs(ph, i):
    return i < B if ph == 1 else i >= 1


def pieces_image(ph, i):
    n = i - 1 if ph == 1 else i + 1
    return n, 0 <= n < B


class Image:

    def __init__(self, first, trip=None):
        self.first, self.trip = first, trip
        self.parity = first % 2

    def __add__(self, k):
        return Image(self.first + k, self.trip)

    @property
    def value(self):
        return self.first if self.trip is None else self.trip * 2 + self.first


def count_increments():
    counts, at = {}, {}

    def inc(sem, key, by=1):
        at[sem] = at.get(sem, 0) + by
        counts[sem, key] = at[sem]

    def side(name, n):
        for step in STEPS[name]:
            inc(CHAIN[name[:2]], (name, n, step))

    inc("x_loaded", ("x", 0), 16)
    inc("x_loaded", ("x", 1), 16)
    for slot in sorted(SIDES_1):
        for name, d in SIDES_1[slot]:
            if name[:2] == "p1":
                side(name, 0)
    for p in range(len(PIECES_1)):
        inc("maxima_ready", (1, 0, p))
        inc("maxima_taken", (1, 0, p))
    side("r1", 0)
    for i in range(0, B + 1):
        for ph in (1, 2):
            n = i if ph == 1 else i - 1
            run = main_runs(ph, i)
            m, there = pieces_image(ph, i)
            if run:
                for u in range(len(UNITS[ph])):
                    inc("scores_ready", (ph, n, u))
                    inc("exp_done", (ph, n, u))
                for t in range(NT):
                    inc("values_done", (ph, n, t))
                    inc("rows_added", (ph, n, t))
                inc("out_copied", (ph, n))
                if ph == 1:
                    inc("bias_added", n)
            if there:
                for p in range(len(PIECES[3 - ph])):
                    inc("maxima_ready", (3 - ph, m, p))
                    inc("maxima_taken", (3 - ph, m, p))
            for slot in sorted(SIDES[ph]):
                for name, d in SIDES[ph][slot]:
                    if 0 <= i + d < B:
                        side(name, i + d)
            if ph == 1 and 0 <= i - 2:
                inc("block_stored", i - 2, 48)
            if ph == 1 and i + 2 < B:
                inc("x_loaded", ("x", i + 2), 16)
    for name in ("f2.rs", "f2.out", "l2", "moe.tr", "moe.lg"):
        side(name, B - 1)
    inc("block_stored", B - 1, 48)
    return counts


COUNTS = count_increments()


def done(sem, *key):
    image = next((k for k in key if isinstance(k, Image)), None)
    flat = lambda n: tuple(n if isinstance(k, Image) else k for k in key)
    at = lambda n: COUNTS[sem, flat(n) if len(key) > 1 else n]
    if image is None:
        return COUNTS[sem, key]
    first = at(image.first)
    if image.trip is None:
        return first
    step = at(image.first + 2) - first
    for k in range(LOOP_TRIPS):
        assert at(image.first + 2 * k) == first + k * step, (sem, key)
    return image.trip * step + first


def earlier(sem, *key, back=1):
    v = done(sem, *key)
    image = next((k for k in key if isinstance(k, Image)), None)
    if isinstance(v, int) and v - back <= 0:
        return []
    return [v - back]


def exists(sem, *key):
    flat = tuple(k.first if isinstance(k, Image) else k for k in key)
    return (sem, flat if len(flat) > 1 else flat[0]) in COUNTS


def build_program(nc, x, out, gn_scale, gn_bias, wq, bq, wk, bk, wv_t, bv, wo, bo,
                  a_wq, a_wk, a_wv_t, gate_t, gate_b, w1, w2, b2_t, group_mean, ident, causal_q, causal_k, block_rows):
    logits_dram = nc.dram_tensor("logits_scratch", (B, E, S), F32, kind="Internal").ap()
    t2_dram = nc.dram_tensor("t2_scratch", (B, P, NT * C), F32, kind="Internal").ap()
    xv = x.rearrange("b (t p) c -> b p t c", p=P)
    outv = out.rearrange("b (t p) c -> b p t c", p=P)
    whole = ExitStack()
    with whole:
        sb = lambda name, shape, dt=F32: whole.enter_context(nc.sbuf_tensor(name, shape, dt))
        u_all = sb("u_all", [P, B, NT * C])
        ident_f = sb("ident_f", [P, P])
        gate_b_sb = sb("gate_b_sb", [2 * E, 1])
        with ExitStack() as ctx:
            attention_part(nc, ctx, locals())
        with ExitStack() as ctx:
            expert_part(nc, ctx, locals())


def attention_part(nc, ctx, g):
    (x, xv, logits_dram, t2_dram, u_all, ident_f, gate_b_sb) = (
        g[k] for k in ("x", "xv", "logits_dram", "t2_dram", "u_all", "ident_f", "gate_b_sb"))

    def sb(name, shape, dt=F32):
        return ctx.enter_context(nc.sbuf_tensor(name, shape, dt))

    def ps(name, shape):
        return ctx.enter_context(nc.psum_tensor(name, shape, F32))

    def sem(name):
        return ctx.enter_context(nc.semaphore(name))

    scores = ps("scores", [P, NST, HALF])
    maxima_in = ps("maxima_in", [P, 2, HALF])
    values_out = ps("values_out", [P, HALF])
    proj_ps = ps("proj_ps", [P, HALF])
    fin_ps = ps("fin_ps", [P, HALF])

    keys = {s: [sb(f"keys{s}{q}", [P, S], F32R) for q in range(2)] for s in (1, 2)}
    keys_hi = {s: [sb(f"keys_hi{s}{q}", [KROWS, S], F32R) for q in range(2)] for s in (1, 2)}
    queries = {s: [sb(f"queries{s}{q}", [P, S], F32R) for q in range(2)] for s in (1, 2)}
    queries_lo = {s: [sb(f"queries_lo{s}{q}", [KROWS, S], F32R) for q in range(2)] for s in (1, 2)}
    probs = sb("probs", [P, NP, S])
    prob_sum = {s: sb(f"prob_sum{s}", [P, S]) for s in (1, 2)}
    maxima = {s: sb(f"maxima{s}", [P, NT, 2]) for s in (1, 2)}
    neg_max = {s: sb(f"neg_max{s}", [P, NT]) for s in (1, 2)}
    x_sb = [sb(f"x_sb{q}", [P, NT, C]) for q in range(2)]
    x_bias = sb("x_bias", [P, NT, C])
    t1 = [sb(f"t1{q}", [P, NT, C]) for q in range(2)]
    t2 = sb("t2", [P, NT, C])
    normed = [sb(f"normed{q}", [P, NT, C]) for q in range(2)]
    u_sb = sb("u_sb", [P, NT, C])
    centred = sb("centred", [P, NT, C])
    squares = sb("squares", [P, NT, C])
    ln = sb("ln", [P, 6, NT])
    xt = sb("xt", [P, HALF])
    h_full = sb("h_full", [P, HALF])
    h_hi = sb("h_hi", [P, HALF], F32R)
    h_stack = sb("h_stack", [P, S], F32R)
    bn = sb("bn", [P, 6])
    gn = sb("gn", [P, 12])
    affine = [sb(f"affine{q}", [P, 2]) for q in range(2)]
    out_raw = sb("out_raw", [P, HALF])
    recip = sb("recip", [P, HALF])
    out_norm = sb("out_norm", [P, HALF])
    ut = sb("ut", [P, HALF])
    logits = sb("logits", [2 * E, S])
    w_raw = {k: sb(f"w_raw_{k}", [P, P]) for k in ("q1", "k1", "m2")}
    w_hi = {k: sb(f"w_hi_{k}", [P, P], F32R) for k in ("q1", "k1", "m2")}
    w_lo = {k: sb(f"w_lo_{k}", [P, P], F32R) for k in ("q1", "k1", "m2")}
    w_out = {s: sb(f"w_out{s}", [P, P]) for s in (1, 2)}
    gate_bd = sb("gate_bd", [P, 2 * E])
    a_w = sb("a_w", [C, 2, P])
    vo = sb("vo", [C, 3, C])
    rows = sb("rows", [1, 2, C])
    bias_out = sb("bias_out", [P, C])
    ones_f = sb("ones_f", [P, P])
    minus_half = sb("minus_half", [P, NT])
    chan = sb("chan", [P, 4])
    bv_col = sb("bv_col", [C, 1])
    group_mean = sb("group_mean_sb", [P, P])
    ident_b = sb("ident_b", [P, P], BF16)
    masks_f = sb("masks_f", [P, 2, P])
    mask_q = sb("mask_q", [P, P], BF16)
    mask_k = sb("mask_k", [P, P], BF16)
    block_rows = sb("block_rows_sb", [KROWS, S])

    names = ["x_loaded", "scores_ready", "exp_done", "values_done", "rows_added", "out_copied", "bias_added",
             "maxima_ready", "maxima_taken", "proj_step", "fin_step", "norm_step", "block_stored",
             "const_loaded", "zeroed", "const_step"]
    (x_loaded, scores_ready, exp_done, values_done, rows_added, out_copied, bias_added, maxima_ready,
     maxima_taken, proj_step, fin_step, norm_step, block_stored, const_loaded, zeroed, const_step) = [
        sem(n) for n in names]
    CONST_DMAS = 0
    block = ctx.enter_context(nc.Block())

    const_loads = []
    for r in range(2):
        for c in range(2):
            const_loads.append((w_raw["q1"][r * C:r * C + C, c * C:c * C + C], g["wq"]))
            const_loads.append((w_raw["k1"][r * C:r * C + C, c * C:c * C + C], g["wk"]))
        const_loads.append((w_out[2][r * C:r * C + C, r * C:r * C + C], g["a_wv_t"]))
        const_loads.append((gate_bd[r * C:r * C + C, r * E:r * E + E], g["gate_t"]))
        const_loads.append((a_w[:, 0, r * C:r * C + C], g["a_wq"]))
        const_loads.append((a_w[:, 1, r * C:r * C + C], g["a_wk"]))
        for k, name in enumerate(("gn_scale", "gn_bias", "bq", "bk")):
            const_loads.append((chan[r * C:r * C + C, k:k + 1], g[name]))
        const_loads.append((gate_b_sb[r * E:r * E + E, :], g["gate_b"]))
    const_loads += [(vo[:, 0, :], g["wv_t"]), (vo[:, 1, :], g["wo"]), (bv_col[:, :], g["bv"]),
                    (rows[:, 0, :], g["bo"]), (group_mean[:, :], g["group_mean"]), (ident_f[:, :], g["ident"]),
                    (masks_f[:, 0, :], g["causal_q"]), (masks_f[:, 1, :], g["causal_k"]),
                    (block_rows[C:KROWS, :], g["block_rows"])]
    ALL_CONST = 16 * len(const_loads)

    def images(i):
        return i

    def iterations(eng, emit):
        for k in range(LOOP_FIRST):
            emit(Image(k))
        with eng.Fori(0, LOOP_TRIPS) as trip:
            emit(Image(LOOP_FIRST, trip))
            emit(Image(LOOP_FIRST + 1, trip))
        for k in range(LOOP_FIRST + 2 * LOOP_TRIPS, LAST + 1):
            emit(Image(k))

    def sides(ph, i, slot):
        for name, d in SIDES[ph].get(slot, []):
            if 0 <= i.first + d < B:
                yield name, i + d

    def pieces(ph, i, slot):
        m, there = pieces_image(ph, i.first)
        if there:
            for p, at in enumerate(PIECE_SLOTS[ph]):
                if at == slot:
                    yield 3 - ph, i + (m - i.first), p

    def slots(ph, i):
        run = main_runs(ph, i.first)
        return [(u, run) for u in range(len(UNITS[ph]))]

    def cols(unit):
        t, a, j0 = unit
        return a * HALF + j0 * P, a * HALF + HALF

    def key_cols(t):
        c = (t % 2) * HALF + (t // 2) * P
        return slice(c, c + P)

    @block.sync
    def _(sp):
        sp.dma_start(x_sb[0][:, :, :], xv[0]).then_inc(x_loaded, 16)
        for dst, src in const_loads:
            sp.dma_start(dst, src).then_inc(const_loaded, 16)
            if dst is const_loads[0][0]:
                pass
        sp.dma_start(x_sb[1][:, :, :], xv[1]).then_inc(x_loaded, 16)

        def held(value):
            return value if isinstance(value, int) else sp.snap(value)

        def image_of(ap, at):
            return ap[at] if isinstance(at, int) else ap[bass.ds(at, 1)].squeeze(0)

        def emit(i):
            if i.first >= 2:
                store(i + (-2))
            if i.first + 2 < B:
                at = held((i + 2).value)
                sp.wait_ge(fin_step, done("fin_step", "f1.out", i, "t"))
                sp.dma_start(x_sb[i.parity][:, :, :], image_of(xv, at)).then_inc(x_loaded, 16)

        def store(n):
            at, normed_u, logits_there = (held(n.value), held(done("norm_step", "l2", n, "v")),
                                          held(done("fin_step", "moe.lg", n, "lg")))
            sp.wait_ge(norm_step, normed_u)
            u_dst = u_all[:, n.value, :] if n.trip is None else u_all[:, bass.ds(at, 1), :].squeeze(1)
            sp.dma_start(u_dst, u_sb[:, :, :].rearrange("p t c -> p (t c)")).then_inc(block_stored, 16)
            sp.dma_start(image_of(t2_dram, at), t2[:, :, :].rearrange("p t c -> p (t c)")).then_inc(block_stored, 16)
            sp.wait_ge(fin_step, logits_there)
            sp.dma_start(image_of(logits_dram, at), logits[0:E, :]).then_inc(block_stored, 16)

        iterations(sp, emit)
        store(Image(B - 1))
        sp.wait_ge(block_stored, 48 * B)

    @block.tensor
    def _(pe):
        def transposes(dst, src):
            for j in range(NJ):
                mm = pe.transpose(dst[:, j * P:(j + 1) * P],
                                  src[:, 2 * j:2 * j + 2, :].rearrange("p t c -> p (t c)"), ident_f[:, :])
            return mm

        def project(w, src, a):
            pe.matmul(proj_ps[:, :], w_lo[w][:, :], src[:, a * HALF:(a + 1) * HALF], start=True, stop=False)
            return pe.matmul(proj_ps[:, :], w_hi[w][:, :], src[:, a * HALF:(a + 1) * HALF], start=False, stop=True)

        def side(name, n):
            q = n.parity
            first = STEPS[name][0]
            if name[:2] in ("p1", "p2"):
                for v in earlier("proj_step", name, n, "tr" if name.endswith("tr") else "mm") if name != "p1.h" else []:
                    pe.wait_ge(proj_step, v)
                if name == "p1.tr":
                    pe.wait_ge(x_loaded, done("x_loaded", "x", n))
                    transposes(proj_ps, x_sb[q]).then_inc(proj_step, 1)
                elif name == "p1.g1":
                    pe.matmul(proj_ps[:, 0:2], group_mean[:, :], gn[:, 0:2], start=True, stop=True).then_inc(proj_step, 1)
                elif name == "p1.g2":
                    pe.matmul(proj_ps[:, 0:2], group_mean[:, :], gn[:, 4:6], start=True, stop=True).then_inc(proj_step, 1)
                elif name in ("p1.qa", "p1.qb"):
                    project("q1", h_stack, int(name == "p1.qb")).then_inc(proj_step, 1)
                elif name in ("p1.ka", "p1.kb"):
                    project("k1", h_stack, int(name == "p1.kb")).then_inc(proj_step, 1)
                elif name == "p2.tr":
                    pe.wait_ge(norm_step, done("norm_step", "l1", n, "v"))
                    transposes(proj_ps, normed[q]).then_inc(proj_step, 1)
                elif name in ("p2.qa", "p2.qb"):
                    project("m2", keys[2][q], int(name == "p2.qb")).then_inc(proj_step, 1)
            elif name in ("f1.rs", "f2.rs"):
                s = int(name[1])
                for v in earlier("fin_step", name, n, "mm"):
                    pe.wait_ge(fin_step, v)
                pe.wait_ge(rows_added, done("rows_added", s, n, NT - 1))
                for a in range(2):
                    mm = pe.matmul(fin_ps[a * C:(a + 1) * C, :], ones_f[:, 0:C], prob_sum[s][:, a * HALF:(a + 1) * HALF],
                                   start=True, stop=True)
                mm.then_inc(fin_step, 1)
            elif name in ("f1.out", "f2.out"):
                s = int(name[1])
                for v in earlier("fin_step", name, n, "mm"):
                    pe.wait_ge(fin_step, v)
                for j in range(NJ):
                    mm = pe.matmul(fin_ps[:, j * P:(j + 1) * P], out_norm[:, j * P:(j + 1) * P], w_out[s][:, :],
                                   start=True, stop=True)
                mm.then_inc(fin_step, 1)
            elif name == "moe.tr":
                for v in earlier("fin_step", name, n, "tr"):
                    pe.wait_ge(fin_step, v)
                pe.wait_ge(norm_step, done("norm_step", "l2", n, "v"))
                transposes(fin_ps, u_sb).then_inc(fin_step, 1)
            elif name == "moe.lg":
                for v in earlier("fin_step", name, n, "mm"):
                    pe.wait_ge(fin_step, v)
                pe.matmul(fin_ps[0:2 * E, :], gate_bd[:, :], ut[:, :], start=True, stop=True).then_inc(fin_step, 1)
            elif name in ("r1", "r2"):
                s = int(name[1])
                for v in earlier("fin_step", name, n, "tr"):
                    pe.wait_ge(fin_step, v)
                pe.matmul(fin_ps[C:KROWS, 0:P], neg_max[s][:, :], ident_f[:, :], start=True, stop=True).then_inc(fin_step, 1)

        def piece(s, n, p):
            c, h, w = PIECES[s][p]
            q = n.parity
            if p == 0:
                pe.wait_ge(proj_step, done("proj_step", "p1.kb" if s == 1 else "p2.qb", n, "k2"))
            for v in earlier("maxima_taken", s, n, p, back=1 if p == 0 else 2):
                pe.wait_ge(maxima_taken, v)
            t = 2 * (c % NJ) + c // NJ
            diagonal = s == 2 and h == t % 2
            if diagonal:
                pe.matmul(maxima_in[:, p % 2, (w - 1) * P:w * P], ident_b[:, :], mask_q[:, :], start=True, stop=True)
            pe.matmul(maxima_in[:, p % 2, 0:w * P], queries[s][q][:, c * P:(c + 1) * P],
                      keys[s][q][:, h * HALF:h * HALF + w * P], start=not diagonal, stop=True,
                      skip_group_check=diagonal).then_inc(maxima_ready, 1)

        def score(s, n, u):
            t, a, j0 = UNITS[s][u]
            q = n.parity
            lo, hi = cols(UNITS[s][u])
            if u == 0:
                pe.wait_ge(fin_step, done("fin_step", f"r{s}", n, "row"))
            for v in earlier("exp_done", s, n, u, back=1 if (s, u) == (1, 0) else NST):
                pe.wait_ge(exp_done, v)
            bank = scores[:, (u + s - 1) % NST, 0:hi - lo]
            diagonal = s == 2 and a == t % 2
            if diagonal:
                pe.matmul(bank[:, 0:P], ident_b[:, :], mask_k[:, :], start=True, stop=True)
            pe.matmul(bank, keys_hi[s][q][:, key_cols(t)], queries_lo[s][q][:, lo:hi], start=not diagonal, stop=False,
                      skip_group_check=diagonal)
            pe.matmul(bank, keys[s][q][:, key_cols(t)], queries[s][q][:, lo:hi], start=False, stop=True,
                      skip_group_check=diagonal).then_inc(scores_ready, 1)

        def values(s, n, t):
            v_sb = x_sb[n.parity] if s == 1 else normed[n.parity]
            us = [u for u, unit in enumerate(UNITS[s]) if unit[0] == t]
            if t == 0:
                for v in earlier("out_copied", s, n):
                    pe.wait_ge(out_copied, v)
            pe.wait_ge(exp_done, done("exp_done", s, n, us[-1]))
            for u in us:
                _, a, j0 = UNITS[s][u]
                lo, hi = cols(UNITS[s][u])
                mm = pe.matmul(values_out[a * C:(a + 1) * C, j0 * P:HALF], v_sb[:, t, :], probs[:, t % NP, lo:hi],
                               start=t == 0, stop=t == NT - 1, skip_group_check=True)
            mm.then_inc(values_done, 1)

        pe.wait_ge(const_loaded, ALL_CONST)
        pe.wait_ge(const_step, 1)
        pe.matmul(fin_ps[0:C, 0:C], vo[:, 0, :], vo[:, 1, :], start=True, stop=True)
        pe.matmul(fin_ps[0:1, C:2 * C], bv_col[:, :], vo[:, 1, :], start=True, stop=True)
        pe.matmul(fin_ps[:, 2 * C:2 * C + P], a_w[:, 0, :], a_w[:, 1, :], start=True, stop=True).then_inc(const_step, 1)
        pe.wait_ge(const_step, 4)
        pe.matmul(fin_ps[:, 0:C], ones_f[0:1, :], rows[:, 1, :], start=True, stop=True).then_inc(const_step, 1)
        pe.wait_ge(const_step, 6)
        pe.wait_ge(zeroed, 3)

        for slot in sorted(SIDES_1):
            for name, d in SIDES_1[slot]:
                if name[:2] == "p1":
                    side(name, Image(0))
        for p in range(len(PIECES_1)):
            piece(1, Image(0), p)
        side("r1", Image(0))

        def emit(i):
            for ph in (1, 2):
                n = i if ph == 1 else i + (-1)
                before = (2, i + (-2)) if ph == 1 else (1, i)
                for u, run in slots(ph, i):
                    if run:
                        score(ph, n, u)
                    if u == 1 and main_runs(3 - ph, i.first if ph == 2 else i.first - 1) and before[1].first >= 0:
                        values(before[0], before[1], NT - 1)
                    if run and u >= 3 and u % 2:
                        values(ph, n, (u - 3) // 2)
                    if run and u == len(UNITS[ph]) - 1 and u % 2 == 0:
                        values(ph, n, NT - 2)
                    for s, m, p in pieces(ph, i, u):
                        piece(s, m, p)
                    for name, m in sides(ph, i, u):
                        side(name, m)

        iterations(pe, emit)
        values(2, Image(B - 1), NT - 1)
        for name in ("f2.rs", "f2.out", "moe.tr", "moe.lg"):
            side(name, Image(B - 1))

    @block.scalar
    def _(act):
        def round_to(dst, src, bias=0.0):
            return nc.scalar.activation(dst, src, ACT.Identity, bias=bias, scale=1.0)

        def side(name, n):
            q = n.parity
            if name == "p1.tr":
                act.wait_ge(proj_step, done("proj_step", name, n, "tr"))
                nc.scalar.copy(xt[:, :], proj_ps[:, :]).then_inc(proj_step, 1)
            elif name == "p1.h":
                act.wait_ge(proj_step, done("proj_step", name, n, "lb"))
                nc.scalar.copy(h_stack[0:C, 0:HALF], h_hi[0:C, :])
                nc.scalar.copy(h_stack[0:C, HALF:S], h_hi[C:P, :]).then_inc(proj_step, 1)
            elif name in ("p1.qa", "p1.qb", "p1.ka", "p1.kb"):
                a = int(name[-1] == "b")
                act.wait_ge(proj_step, done("proj_step", name, n, "mm"))
                dst, b = (queries[1][q], 2) if name[3] == "q" else (keys[1][q], 3)
                round_to(dst[:, a * HALF:(a + 1) * HALF], proj_ps[:, :], chan[:, b:b + 1]).then_inc(proj_step, 1)
            elif name == "p2.tr":
                act.wait_ge(proj_step, done("proj_step", name, n, "tr"))
                nc.scalar.copy(h_hi[:, :], proj_ps[:, :]).then_inc(proj_step, 1)
                nc.scalar.copy(keys[2][q][0:C, 0:HALF], proj_ps[0:C, :])
                nc.scalar.copy(keys[2][q][0:C, HALF:S], proj_ps[C:P, :]).then_inc(proj_step, 1)
            elif name in ("p2.qa", "p2.qb"):
                a = int(name[-1] == "b")
                act.wait_ge(proj_step, done("proj_step", name, n, "mm"))
                nc.scalar.copy(queries[2][q][:, a * HALF:(a + 1) * HALF], proj_ps[:, :]).then_inc(proj_step, 1)
            elif name in ("l1", "l2"):
                act.wait_ge(norm_step, done("norm_step", name, n, "xc"))
                nc.scalar.activation(squares[:, :, :], centred[:, :, :], ACT.Square).then_inc(norm_step, 1)
            elif name == "moe.tr":
                act.wait_ge(fin_step, done("fin_step", name, n, "tr"))
                nc.scalar.copy(ut[:, :], fin_ps[:, :]).then_inc(fin_step, 1)
            elif name == "moe.lg":
                act.wait_ge(fin_step, done("fin_step", name, n, "mm"))
                if exists("block_stored", n + (-1)):
                    act.wait_ge(block_stored, done("block_stored", n + (-1)))
                for a in range(2):
                    mm = nc.scalar.activation(
                        logits[0:E, :].rearrange("e (j a t) -> e j a t", a=2, t=P)[:, :, a, :],
                        fin_ps[a * E:(a + 1) * E, :].rearrange("e (j t) -> e j t", t=P), ACT.Identity,
                        bias=gate_b_sb[a * E:(a + 1) * E, :], scale=1.0)
                mm.then_inc(fin_step, 1)

        def exponentials(s, n, u):
            t, a, j0 = UNITS[s][u]
            lo, hi = cols(UNITS[s][u])
            if u == 0 or UNITS[s][u - 1][0] != t:
                for v in earlier("values_done", s, n, t, back=NP):
                    act.wait_ge(values_done, v)
                for v in earlier("rows_added", s, n, t, back=NP):
                    act.wait_ge(rows_added, v)
            act.wait_ge(scores_ready, done("scores_ready", s, n, u))
            nc.scalar.activation(probs[:, t % NP, lo:hi], scores[:, (u + s - 1) % NST, 0:hi - lo], ACT.Exp,
                                 scale=SCALE).then_inc(exp_done, 1)

        def copy_out(s, n):
            act.wait_ge(values_done, done("values_done", s, n, NT - 1))
            other = ("f2.rs", n + (-2)) if s == 1 else ("f1.rs", n + 1)
            if exists("fin_step", other[0], other[1], "on"):
                act.wait_ge(fin_step, done("fin_step", other[0], other[1], "on"))
            nc.scalar.copy(out_raw[:, :], values_out[:, :]).then_inc(out_copied, 1)

        act.wait_ge(const_step, 2)
        nc.scalar.copy(w_out[1][0:C, 0:C], fin_ps[0:C, 0:C])
        nc.scalar.copy(w_out[1][C:P, C:P], fin_ps[0:C, 0:C])
        nc.scalar.copy(w_raw["m2"][:, :], fin_ps[:, 2 * C:2 * C + P])
        nc.scalar.activation(rows[:, 1, :], fin_ps[0:1, C:2 * C], ACT.Copy).then_inc(const_step, 1)
        act.wait_ge(const_step, 5)
        nc.scalar.copy(bias_out[:, :], fin_ps[:, 0:C]).then_inc(const_step, 1)
        act.wait_ge(const_loaded, ALL_CONST)

        for slot in sorted(SIDES_1):
            for name, d in SIDES_1[slot]:
                if name[:2] == "p1":
                    side(name, Image(0))

        def emit(i):
            for ph in (1, 2):
                n = i if ph == 1 else i + (-1)
                before = (2, i + (-2)) if ph == 1 else (1, i)
                for u, run in slots(ph, i):
                    if run:
                        exponentials(ph, n, u)
                    if u == 1 and main_runs(3 - ph, i.first if ph == 2 else i.first - 1) and before[1].first >= 0:
                        copy_out(*before)
                    for name, m in sides(ph, i, u):
                        side(name, m)

        iterations(act, emit)
        copy_out(2, Image(B - 1))
        for name in ("f2.rs", "f2.out", "l2", "moe.tr", "moe.lg"):
            side(name, Image(B - 1))

    @block.gpsimd
    def _(pool):
        def side(name, n):
            if name == "p1.g2":
                pool.wait_ge(proj_step, done("proj_step", name, n, "ve"))
                nc.gpsimd.tensor_tensor(gn[:, 7:8], gn[:, 6:7], minus_half[:, 0:1], ALU.pow).then_inc(proj_step, 1)
            elif name in ("l1", "l2"):
                src, dst = (t1[n.parity], normed[n.parity]) if name == "l1" else (t2, u_sb)
                pool.wait_ge(norm_step, done("norm_step", name, n, "nm"))
                nc.gpsimd.tensor_tensor(centred[:, :, :], src[:, :, :], ln[:, 1, :].unsqueeze(2).to_broadcast([P, NT, C]),
                                        ALU.add).then_inc(norm_step, 1)
                pool.wait_ge(norm_step, done("norm_step", name, n, "ve"))
                nc.gpsimd.tensor_tensor(ln[:, 4, :], ln[:, 3, :], minus_half[:, :], ALU.pow).then_inc(norm_step, 1)
                pool.wait_ge(norm_step, done("norm_step", name, n, "rs"))
                if name == "l1" and exists("values_done", 2, n + (-2), NT - 1):
                    pool.wait_ge(values_done, done("values_done", 2, n + (-2), NT - 1))
                if name == "l2" and exists("block_stored", n + (-1)):
                    pool.wait_ge(block_stored, done("block_stored", n + (-1)))
                nc.gpsimd.tensor_tensor(dst[:, :, :], centred[:, :, :], ln[:, 4, :].unsqueeze(2).to_broadcast([P, NT, C]),
                                        ALU.mult).then_inc(norm_step, 1)

        def add_rows(s, n, t):
            us = [u for u, unit in enumerate(UNITS[s]) if unit[0] == t]
            total, new = prob_sum[s], probs[:, t % NP, :]
            if t == 0:
                return
            pool.wait_ge(exp_done, done("exp_done", s, n, us[-1]))
            if t == 1:
                if exists("fin_step", f"f{s}.rs", n + (-1), "mm"):
                    pool.wait_ge(fin_step, done("fin_step", f"f{s}.rs", n + (-1), "mm"))
                lo = 0 if s == 1 else P
                if lo:
                    nc.gpsimd.tensor_tensor(total[:, 0:lo], probs[:, 0, 0:lo], ones_f[:, 0:lo], ALU.mult)
                nc.gpsimd.tensor_tensor(total[:, lo:], probs[:, 0, lo:], new[:, lo:], ALU.add).then_inc(rows_added, 2)
                return
            pool.wait_ge(rows_added, done("rows_added", s, n, t - 1))
            los = [cols(UNITS[s][u]) for u in us]
            if len(los) == 2 and los[0][0] + HALF == los[1][0]:
                w = HALF - los[0][0]
                view = lambda ap: ap.rearrange("p (a c) -> p a c", a=2)[:, :, HALF - w:HALF]
                nc.gpsimd.tensor_tensor(view(total[:, :]), view(total[:, :]), view(new), ALU.add).then_inc(rows_added, 1)
            else:
                for lo, hi in los:
                    ins = nc.gpsimd.tensor_tensor(total[:, lo:hi], total[:, lo:hi], new[:, lo:hi], ALU.add)
                ins.then_inc(rows_added, 1)

        def add_bias(n):
            pool.wait_ge(x_loaded, done("x_loaded", "x", n))
            if exists("fin_step", "f1.out", n + (-1), "t"):
                pool.wait_ge(fin_step, done("fin_step", "f1.out", n + (-1), "t"))
            nc.gpsimd.tensor_tensor(x_bias[:, :, :], x_sb[n.parity][:, :, :],
                                    bias_out[:, :].unsqueeze(1).to_broadcast([P, NT, C]), ALU.add).then_inc(bias_added, 1)

        nc.gpsimd.memset(minus_half[:, :], -0.5)
        nc.gpsimd.memset(ones_f[:, :], 1.0).then_inc(zeroed, 1)
        pool.wait_ge(zeroed, 1)
        pool.wait_ge(const_step, 6)
        for slot in sorted(SIDES_1):
            for name, d in SIDES_1[slot]:
                if name[:2] == "p1":
                    side(name, Image(0))

        def emit(i):
            for ph in (1, 2):
                n = i if ph == 1 else i + (-1)
                before = (2, i + (-2)) if ph == 1 else (1, i)
                for u, run in slots(ph, i):
                    if u == 1 and main_runs(3 - ph, i.first if ph == 2 else i.first - 1) and before[1].first >= 0:
                        add_rows(before[0], before[1], NT - 1)
                    if run and u >= 3 and u % 2:
                        add_rows(ph, n, (u - 3) // 2)
                    if run and u == len(UNITS[ph]) - 1 and u % 2 == 0:
                        add_rows(ph, n, NT - 2)
                    if ph == 1 and run and u == 12:
                        add_bias(i)
                    for name, m in sides(ph, i, u):
                        side(name, m)

        iterations(pool, emit)
        add_rows(2, Image(B - 1), NT - 1)
        side("l2", Image(B - 1))

    @block.vector
    def _(dve):
        V = nc.vector

        def side(name, n):
            q = n.parity

            def step(chain, sem_, step_name):
                for v in earlier(chain, name, n, step_name):
                    dve.wait_ge(sem_, v)

            if name == "p1.tr":
                step("proj_step", proj_step, "bn")
                V.bn_stats(bn[:, :], xt[:, :]).then_inc(proj_step, 1)
                step("proj_step", proj_step, "ag")
                V.memset(gn[:, 11:12], 0.0)
                V.bn_aggr(gn[:, 0:2], bn[:, :]).then_inc(proj_step, 1)
            elif name == "p1.g1":
                step("proj_step", proj_step, "gv")
                V.tensor_copy(gn[:, 2:4], proj_ps[:, 0:2]).then_inc(proj_step, 1)
                step("proj_step", proj_step, "d")
                V.tensor_scalar(gn[:, 4:6], gn[:, 0:2], gn[:, 2:3], None, ALU.subtract).then_inc(proj_step, 1)
                step("proj_step", proj_step, "d2")
                V.tensor_tensor(gn[:, 4:6], gn[:, 4:6], gn[:, 4:6], ALU.mult).then_inc(proj_step, 1)
            elif name == "p1.g2":
                step("proj_step", proj_step, "ve")
                V.scalar_tensor_tensor(out=gn[:, 6:7], in0=proj_ps[:, 0:1], scalar=EPS_GN, in1=gn[:, 3:4],
                                       op0=ALU.add, op1=ALU.add).then_inc(proj_step, 1)
                step("proj_step", proj_step, "a")
                V.tensor_tensor(affine[q][:, 0:1], gn[:, 7:8], chan[:, 0:1], ALU.mult).then_inc(proj_step, 1)
                step("proj_step", proj_step, "ma")
                V.tensor_tensor(gn[:, 8:9], gn[:, 2:3], affine[q][:, 0:1], ALU.mult).then_inc(proj_step, 1)
                step("proj_step", proj_step, "b")
                V.tensor_tensor(affine[q][:, 1:2], chan[:, 1:2], gn[:, 8:9], ALU.subtract).then_inc(proj_step, 1)
            elif name == "p1.h":
                step("proj_step", proj_step, "hf")
                V.tensor_scalar(h_full[:, :], xt[:, :], affine[q][:, 0:1], affine[q][:, 1:2], ALU.mult,
                                ALU.add).then_inc(proj_step, 1)
                step("proj_step", proj_step, "hh")
                V.tensor_copy(h_hi[:, :], h_full[:, :]).then_inc(proj_step, 1)
                step("proj_step", proj_step, "la")
                V.tensor_tensor(h_stack[C:P, 0:HALF], h_full[0:C, :], h_hi[0:C, :], ALU.subtract).then_inc(proj_step, 1)
                V.tensor_tensor(h_stack[C:P, HALF:S], h_full[C:P, :], h_hi[C:P, :], ALU.subtract).then_inc(proj_step, 1)
            elif name in ("p1.qa", "p1.qb"):
                c = slice(HALF * (name[-1] == "b"), HALF * (name[-1] == "b") + HALF)
                step("proj_step", proj_step, "lo")
                V.scalar_tensor_tensor(out=queries_lo[1][q][0:C, c], in0=proj_ps[0:C, :], scalar=chan[0:C, 2:3],
                                       in1=queries[1][q][0:C, c], op0=ALU.add, op1=ALU.subtract).then_inc(proj_step, 1)
            elif name in ("p1.ka", "p1.kb"):
                c = slice(HALF * (name[-1] == "b"), HALF * (name[-1] == "b") + HALF)
                step("proj_step", proj_step, "lo")
                V.scalar_tensor_tensor(out=keys[1][q][C:P, c], in0=proj_ps[C:P, :], scalar=chan[C:P, 3:4],
                                       in1=keys[1][q][C:P, c], op0=ALU.add, op1=ALU.subtract).then_inc(proj_step, 1)
                if name == "p1.kb":
                    V.tensor_copy(keys_hi[1][q][0:C, :], keys[1][q][0:C, :]).then_inc(proj_step, 1)
            elif name == "p2.tr":
                step("proj_step", proj_step, "lo")
                V.tensor_tensor(keys[2][q][C:P, 0:HALF], proj_ps[0:C, :], h_hi[0:C, :], ALU.subtract)
                V.tensor_tensor(keys[2][q][C:P, HALF:S], proj_ps[C:P, :], h_hi[C:P, :], ALU.subtract).then_inc(proj_step, 1)
            elif name in ("p2.qa", "p2.qb"):
                c = slice(HALF * (name[-1] == "b"), HALF * (name[-1] == "b") + HALF)
                step("proj_step", proj_step, "lo")
                V.tensor_tensor(queries_lo[2][q][0:C, c], proj_ps[0:C, :], queries[2][q][0:C, c],
                                ALU.subtract).then_inc(proj_step, 1)
                if name == "p2.qb":
                    V.tensor_copy(keys_hi[2][q][0:C, :], keys[2][q][0:C, :]).then_inc(proj_step, 1)
            elif name in ("f1.rs", "f2.rs"):
                s = int(name[1])
                step("fin_step", fin_step, "ri")
                V.reciprocal(recip[:, :], fin_ps[:, :]).then_inc(fin_step, 1)
                dve.wait_ge(out_copied, done("out_copied", s, n))
                step("fin_step", fin_step, "on")
                V.tensor_tensor(out_norm[:, :], out_raw[:, :], recip[:, :], ALU.mult).then_inc(fin_step, 1)
                if s == 1:
                    step("fin_step", fin_step, "aff")
                    V.tensor_scalar(out_norm[:, :], out_norm[:, :], affine[q][:, 0:1], affine[q][:, 1:2], ALU.mult,
                                    ALU.add).then_inc(fin_step, 1)
            elif name == "f1.out":
                step("fin_step", fin_step, "t")
                dve.wait_ge(bias_added, done("bias_added", n))
                V.tensor_tensor(t1[q][:, :, :].rearrange("p t c -> p (t c)"), fin_ps[:, :],
                                x_bias[:, :, :].rearrange("p t c -> p (t c)"), ALU.add).then_inc(fin_step, 1)
            elif name == "f2.out":
                step("fin_step", fin_step, "t")
                if exists("block_stored", n + (-1)):
                    dve.wait_ge(block_stored, done("block_stored", n + (-1)))
                V.tensor_tensor(t2[:, :, :].rearrange("p t c -> p (t c)"), fin_ps[:, :],
                                t1[q][:, :, :].rearrange("p t c -> p (t c)"), ALU.add).then_inc(fin_step, 1)
            elif name in ("l1", "l2"):
                src = t1[q] if name == "l1" else t2
                dve.wait_ge(fin_step, done("fin_step", f"f{name[1]}.out", n, "t"))
                step("norm_step", norm_step, "sum")
                V.reduce_sum(ln[:, 0, :], src[:, :, :], AX.X).then_inc(norm_step, 1)
                step("norm_step", norm_step, "nm")
                V.tensor_scalar(ln[:, 1, :], ln[:, 0, :], -1.0 / C, None, ALU.mult).then_inc(norm_step, 1)
                step("norm_step", norm_step, "vs")
                V.reduce_sum(ln[:, 2, :], squares[:, :, :], AX.X).then_inc(norm_step, 1)
                step("norm_step", norm_step, "ve")
                V.tensor_scalar(ln[:, 3, :], ln[:, 2, :], 1.0 / C, EPS_LN, ALU.mult, ALU.add).then_inc(norm_step, 1)
            elif name in ("r1", "r2"):
                s = int(name[1])
                dve.wait_ge(maxima_taken, done("maxima_taken", s, n, len(PIECES[s]) - 1))
                step("fin_step", fin_step, "neg")
                V.tensor_reduce(neg_max[s][:, :], maxima[s][:, :, :], AX.X, ALU.max, negate=True).then_inc(fin_step, 1)
                step("fin_step", fin_step, "row")
                V.tensor_tensor(
                    queries_lo[s][q][C:KROWS, :].rearrange("r (c t) -> r c t", t=P),
                    fin_ps[C:KROWS, 0:P].unsqueeze(1).to_broadcast([NT, NT, P]),
                    block_rows[C:KROWS, :].rearrange("r (c t) -> r c t", t=P), ALU.mult).then_inc(fin_step, 1)

        def piece(s, n, p):
            c, h, w = PIECES[s][p]
            dve.wait_ge(maxima_ready, done("maxima_ready", s, n, p))
            V.reduce_max(maxima[s][:, c, h:h + 1], maxima_in[:, p % 2, 0:w * P], AX.X).then_inc(maxima_taken, 1)

        V.memset(w_out[1][:, :], 0.0)
        V.memset(w_out[2][0:C, C:P], 0.0)
        V.memset(w_out[2][C:P, 0:C], 0.0)
        V.memset(gate_bd[0:C, E:2 * E], 0.0)
        V.memset(gate_bd[C:P, 0:E], 0.0)
        V.memset(maxima[2][:, :, :], NEG_HUGE)
        for s in (1, 2):
            for q in range(2):
                V.memset(keys_hi[s][q][C:KROWS, :].bitcast(F32), 1.0)
        dve.wait_ge(zeroed, 1)
        dve.wait_ge(const_loaded, ALL_CONST)
        V.tensor_copy(ident_b[:, :], ident_f[:, :])
        V.tensor_copy(mask_q[:, :], masks_f[:, 0, :])
        V.tensor_copy(mask_k[:, :], masks_f[:, 1, :]).then_inc(const_step, 1)
        dve.wait_ge(const_step, 3)
        V.tensor_tensor(rows[:, 1, :], rows[:, 1, :], rows[:, 0, :], ALU.add).then_inc(const_step, 1)
        for k in ("q1", "k1", "m2"):
            ins = V.tensor_copy(w_hi[k][:, :], w_raw[k][:, :])
        ins.then_inc(zeroed, 1)
        dve.wait_ge(zeroed, 2)
        for k in ("q1", "k1", "m2"):
            ins = V.tensor_tensor(w_lo[k][:, :], w_raw[k][:, :], w_hi[k][:, :], ALU.subtract)
        ins.then_inc(zeroed, 1)

        for slot in sorted(SIDES_1):
            for name, d in SIDES_1[slot]:
                if name[:2] == "p1":
                    side(name, Image(0))
        for p in range(len(PIECES_1)):
            piece(1, Image(0), p)
        side("r1", Image(0))

        def emit(i):
            for ph in (1, 2):
                for u, run in slots(ph, i):
                    for s, m, p in pieces(ph, i, u):
                        piece(s, m, p)
                    for name, m in sides(ph, i, u):
                        side(name, m)

        iterations(dve, emit)
        for name in ("f2.rs", "f2.out", "l2"):
            side(name, Image(B - 1))


def expert_part(nc, ctx, g):
    (outv, logits_dram, t2_dram, u_all, ident_f) = (g[k] for k in ("outv", "logits_dram", "t2_dram", "u_all", "ident_f"))
    NG = B // BG

    def sb(name, shape, dt=F32):
        return ctx.enter_context(nc.sbuf_tensor(name, shape, dt))

    def ps(name, shape):
        return ctx.enter_context(nc.psum_tensor(name, shape, F32))

    def sem(name):
        return ctx.enter_context(nc.semaphore(name))

    lg = sb("lg", [P, NG, S])
    top = sb("top", [P, NG, TOPK])
    stat = sb("stat", [P, NG, 3])
    ex = sb("ex", [P, 2, S])
    rest = sb("rest", [P, S])
    chosen = sb("chosen", [P, S])
    gates = sb("gates", [P, NG, S])
    gates_t = sb("gates_t", [P, 2, NT, P])
    pooled = sb("pooled", [C + 1, E, B])
    w1_sb = sb("w1_sb", [C + 1, E, HID])
    w2_sb = sb("w2_sb", [P, E, 2, C])
    b2_sb = sb("b2_sb", [C, E])
    hidden = sb("hidden", [P, E, 2, B])
    gathered = sb("gathered", [C, NG, BG, E])
    by_image = sb("by_image", [P, BG, BG, C])
    t2_sb = sb("t2_sb", [P, 2, BG, NT, C])
    out_sb = sb("out_sb", [P, 2, BG, NT, C])

    turn = ps("turn", [P, 2, HALF])
    pool_ps = ps("pool_ps", [P, 2, E])
    hidden_ps = ps("hidden_ps", [P, 2, HALF])
    small_ps = ps("small_ps", [P, HALF])
    add_ps = ps("add_ps", [P, 2, HALF])

    logits_loaded = [sem(f"logits_loaded{k}") for k in range(NG)]
    t2_loaded = [sem(f"t2_loaded{k}") for k in range(NG)]
    out_stored = [sem(f"out_stored{k}") for k in range(NG)]
    (weights_loaded, topk_step, exp_ready, gates_ready, turned, turn_copied, pool_ready,
     pool_copied, hidden_ready, gelu_done, out_ready, out_biased, image_turned, image_copied, ones_set, sum_ready,
     sum_taken) = [sem(n) for n in (
        "weights_loaded", "topk_step", "exp_ready", "gates_ready", "turned",
        "turn_copied", "pool_ready", "pool_copied", "hidden_ready", "gelu_done", "out_ready", "out_biased",
        "image_turned", "image_copied", "ones_set", "sum_ready", "sum_taken")]
    block = ctx.enter_context(nc.Block())

    def store(sp, k):
        sp.wait_ge(sum_taken, NT // 2 * (k + 1))
        for b in range(BG):
            sp.dma_start(outv[k * BG + b], out_sb[:, k % 2, b, :, :]).then_inc(out_stored[k], 16)

    @block.sync
    def _(sp):
        for k in range(NG):
            sp.dma_start(lg[:, k, :], logits_dram[k * BG:(k + 1) * BG].rearrange("b e s -> (b e) s")).then_inc(logits_loaded[k], 16)
        sp.dma_start(w1_sb[:, :, :], g["w1"].rearrange("e d h -> d e h")).then_inc(weights_loaded, 16)
        for half in range(2):
            sp.dma_start(w2_sb[:, :, half, :], g["w2"][:, half * P:(half + 1) * P, :].rearrange("e h o -> h e o")).then_inc(weights_loaded, 16)
        sp.dma_start(b2_sb[:, :], g["b2_t"]).then_inc(weights_loaded, 16)
        for k in range(NG):
            if k >= 2:
                sp.wait_ge(sum_taken, NT // 2 * (k - 1))
            for b in range(BG):
                sp.dma_start(t2_sb[:, k % 2, b, :, :].rearrange("p t c -> p (t c)"), t2_dram[k * BG + b]).then_inc(t2_loaded[k], 16)
            if k >= 1:
                store(sp, k - 1)
        store(sp, NG - 1)
        for k in range(NG):
            sp.wait_ge(out_stored[k], 16 * BG)

    @block.tensor
    def _(pe):
        for k in range(NG):
            pe.wait_ge(gates_ready, k + 1)
            for r in range(2):
                if 2 * k + r >= 2:
                    pe.wait_ge(turn_copied, 2 * k + r - 1)
                for t in range(4):
                    mm = pe.transpose(turn[:, r, t * P:(t + 1) * P], gates[:, k, (4 * r + t) * P:(4 * r + t + 1) * P], ident_f[:, :])
                mm.then_inc(turned, 1)
            pe.wait_ge(turn_copied, 2 * k + 2)
            if k >= 1:
                pe.wait_ge(pool_copied, k)
            for pair in range(BG // 2):
                for t in range(NT):
                    for odd in range(2):
                        b = 2 * pair + odd
                        mm = pe.matmul(pool_ps[odd * C:(odd + 1) * C, pair, :], u_all[:, k * BG + b, t * C:(t + 1) * C],
                                       gates_t[:, k % 2, t, b * E:(b + 1) * E], start=t == 0, stop=t == NT - 1,
                                       skip_group_check=True)
            mm.then_inc(pool_ready, 1)
        pe.wait_ge(weights_loaded, 64)
        pe.wait_ge(ones_set, 1)
        pe.wait_ge(pool_copied, NG)
        for e in range(E):
            for half in range(2):
                at = (e % (E // 2)) * 2 + half
                mm = pe.matmul(hidden_ps[:, e // (E // 2), at * B:(at + 1) * B], w1_sb[:, e, half * P:(half + 1) * P],
                               pooled[:, e, :], start=True, stop=True)
            if e % (E // 2) == E // 2 - 1:
                mm.then_inc(hidden_ready, 1)
        for e in range(E):
            if e % (E // 2) == 0:
                pe.wait_ge(gelu_done, e // (E // 2) + 1)
            for half in range(2):
                mm = pe.matmul(small_ps[0:C, e * B:(e + 1) * B], w2_sb[:, e, half, :], hidden[:, e, half, :],
                               start=half == 0, stop=half == 1)
        mm.then_inc(out_ready, 1)
        pe.wait_ge(out_biased, 1)
        for k in range(NG):
            mm = pe.transpose(turn[:, 0, k * C:(k + 1) * C],
                              gathered[:, k, :, :].rearrange("c b e -> c (b e)"), ident_f[0:C, 0:C])
        mm.then_inc(image_turned, 1)
        pe.wait_ge(image_copied, 1)
        for k in range(NG):
            for r in range(NT // 2):
                n = k * (NT // 2) + r
                if n >= 2:
                    pe.wait_ge(sum_taken, n - 1)
                for t in range(2):
                    mm = pe.matmul(add_ps[:, n % 2, t * BG * C:(t + 1) * BG * C], gates[:, k, (2 * r + t) * P:(2 * r + t + 1) * P],
                                   by_image[:, k, :, :].rearrange("p b c -> p (b c)"), start=True, stop=True)
                mm.then_inc(sum_ready, 1)

    def copies(act, k):
        for r in range(2):
            act.wait_ge(turned, 2 * k + r + 1)
            if k >= 2 and r == 0:
                act.wait_ge(pool_ready, k - 1)
            nc.scalar.copy(gates_t[:, k % 2, 4 * r:4 * r + 4, :].rearrange("p t g -> p (t g)"), turn[:, r, :]).then_inc(turn_copied, 1)
        act.wait_ge(pool_ready, k + 1)
        for odd in range(2):
            for pair in range(BG // 2):
                b = k * BG + 2 * pair + odd
                ins = nc.scalar.copy(pooled[0:C, :, b:b + 1].rearrange("c e o -> c (e o)"), pool_ps[odd * C:(odd + 1) * C, pair, :])
        ins.then_inc(pool_copied, 1)

    @block.scalar
    def _(act):
        for k in range(NG):
            act.wait_ge(topk_step, 5 * k + 2)
            if k >= 2:
                act.wait_ge(gates_ready, k - 1)
            nc.scalar.activation(ex[:, k % 2, :], lg[:, k, :], ACT.Exp, bias=stat[:, k, 0:1], scale=1.0,
                                 accum_out=stat[:, k, 1:2]).then_inc(exp_ready, 1)
            if k >= 1:
                copies(act, k - 1)
        copies(act, NG - 1)
        for h in range(2):
            act.wait_ge(hidden_ready, h + 1)
            nc.scalar.activation(hidden[:, h * (E // 2):(h + 1) * (E // 2), :, :].rearrange("p e h b -> p (e h b)"),
                                 hidden_ps[:, h, :], ACT.Gelu).then_inc(gelu_done, 1)

    @block.vector
    def _(dve):
        V = nc.vector
        V.memset(pooled[C:C + 1, :, :], 1.0)
        V.memset(by_image[:, :, :, :], 0.0).then_inc(ones_set, 1)
        for k in range(NG):
            dve.wait_ge(logits_loaded[k], 16)
            V.max(top[:, k, :], lg[:, k, :]).then_inc(topk_step, 1)
            dve.wait_ge(topk_step, 5 * k + 1)
            V.tensor_scalar(stat[:, k, 0:1], top[:, k, 0:1], -1.0, None, ALU.mult).then_inc(topk_step, 1)
            V.match_replace(rest[:, :], top[:, k, :], lg[:, k, :], NEG_HUGE).then_inc(topk_step, 1)
            dve.wait_ge(topk_step, 5 * k + 3)
            V.tensor_tensor(chosen[:, :], lg[:, k, :], rest[:, :], ALU.not_equal).then_inc(topk_step, 1)
            dve.wait_ge(exp_ready, k + 1)
            V.reciprocal(stat[:, k, 2:3], stat[:, k, 1:2]).then_inc(topk_step, 1)
            dve.wait_ge(topk_step, 5 * k + 5)
            V.scalar_tensor_tensor(out=gates[:, k, :], in0=ex[:, k % 2, :], scalar=stat[:, k, 2:3], in1=chosen[:, :],
                                   op0=ALU.mult, op1=ALU.mult).then_inc(gates_ready, 1)
        dve.wait_ge(out_ready, 1)
        dve.wait_ge(weights_loaded, 64)
        V.tensor_tensor(gathered[:, :, :, :].rearrange("c k b e -> c e (k b)"), small_ps[0:C, :].rearrange("c (e b) -> c e b", b=B),
                        b2_sb[:, :].unsqueeze(2).to_broadcast([C, E, B]), ALU.add).then_inc(out_biased, 1)
        dve.wait_ge(image_turned, 1)
        for b in range(BG):
            r = slice(b * E, (b + 1) * E)
            ins = V.tensor_copy(by_image[r, :, b, :], turn[r, 0, 0:NG * C].rearrange("p (k c) -> p k c", c=C))
        ins.then_inc(image_copied, 1)
        for k in range(NG):
            dve.wait_ge(t2_loaded[k], 16 * BG)
            if k >= 2:
                dve.wait_ge(out_stored[k - 2], 16 * BG)
            for r in range(NT // 2):
                n = k * (NT // 2) + r
                dve.wait_ge(sum_ready, n + 1)
                V.tensor_tensor(out_sb[:, k % 2, :, 2 * r:2 * r + 2, :].rearrange("p b t c -> p t b c"),
                                add_ps[:, n % 2, :].rearrange("p (t b c) -> p t b c", t=2, b=BG),
                                t2_sb[:, k % 2, :, 2 * r:2 * r + 2, :].rearrange("p b t c -> p t b c"), ALU.add).then_inc(sum_taken, 1)


def kernel(x, L0_conv_gn_scale, L0_conv_gn_bias, L0_conv_wq, L0_conv_bq, L0_conv_wk, L0_conv_bk, L0_conv_wv,
           L0_conv_bv, L0_conv_wo, L0_conv_bo, L1_attn_Wq, L1_attn_Wk, L1_attn_Wv, L1_ffn_gate_w, L1_ffn_gate_b,
           L1_ffn_weight1, L1_ffn_weight2):
    import concourse.bacc as bacc
    from concourse.bass_utils import run_bass_kernel_spmd

    asnp = lambda a: np.ascontiguousarray(np.asarray(a))
    column = lambda a: asnp(a).reshape(-1, 1)
    p = np.arange(P)
    same = (p[:, None] % C) // GROUP == (p[None, :] % C) // GROUP
    group_mean = (same / (2.0 * GROUP)).astype(np.float32)
    ident = np.eye(P, dtype=np.float32)
    causal_q = np.where(p[None, :] > p[:, None], MASKED, 0.0).astype(np.float32)
    block_rows = (np.arange(S)[None, :] // P == np.arange(NT)[:, None]).astype(np.float32)
    arrays = {
        "x": asnp(x).reshape(B, S, C),
        "gn_scale": column(L0_conv_gn_scale), "gn_bias": column(L0_conv_gn_bias),
        "wq": asnp(L0_conv_wq), "bq": column(L0_conv_bq), "wk": asnp(L0_conv_wk), "bk": column(L0_conv_bk),
        "wv_t": asnp(np.asarray(L0_conv_wv).T), "bv": column(L0_conv_bv),
        "wo": asnp(L0_conv_wo), "bo": asnp(L0_conv_bo).reshape(1, C),
        "a_wq": asnp(L1_attn_Wq), "a_wk": asnp(L1_attn_Wk), "a_wv_t": asnp(np.asarray(L1_attn_Wv).T),
        "gate_t": asnp(np.asarray(L1_ffn_gate_w).T), "gate_b": column(L1_ffn_gate_b),
        "w1": asnp(L1_ffn_weight1), "w2": asnp(L1_ffn_weight2),
        "b2_t": asnp(np.asarray(L1_ffn_weight2)[:, HID, :].T),
        "group_mean": group_mean, "ident": ident, "causal_q": causal_q, "causal_k": asnp(causal_q.T),
        "block_rows": block_rows,
    }
    nc = bacc.Bacc("TRN2", target_bir_lowering=False, num_devices=1)
    aps = {k: nc.dram_tensor(f"in_{k}", v.shape, mybir.dt.from_np(v.dtype), kind="ExternalInput").ap()
           for k, v in arrays.items()}
    out = nc.dram_tensor("out", (B, S, C), F32, kind="ExternalOutput").ap()
    build_program(nc, out=out, **aps)
    r = run_bass_kernel_spmd(nc, [{f"in_{k}": v for k, v in arrays.items()}], core_ids=[0])
    return r.results[0]["out"].reshape(B, 32, 32, C)
```

```python
from contextlib import ExitStack

import numpy as np

import concourse.bass as bass
from concourse import mybir

ALU = mybir.AluOpType
ACT = mybir.ActivationFunctionType
AX = mybir.AxisListType
F32 = mybir.dt.float32
F32R = mybir.dt.float32r
BF16 = mybir.dt.bfloat16

B, S, C = 16, 1024, 64
P = 128
NT = S // P
NJ = NT // 2
HALF = S // 2
E, HID, TOPK = 32, 256, 8
GROUP = 4
SCALE = float(C) ** -0.5
EPS_GN, EPS_LN = 1e-6, 1e-5
MASKED = -1e30
KROWS = C + NT
NEG_HUGE = -3e38
NST, NM, NP = 2, 3, 4
BG = 4

UNITS_1 = [(t, a, 0) for t in range(NT) for a in range(2)]
UNITS_2 = [(t, a, j0) for t in range(NT) for a, j0 in ((0, (t + 1) // 2), (1, t // 2)) if j0 < NJ]
UNITS = {1: UNITS_1, 2: UNITS_2}
PIECES_1 = [(c, h, NJ) for c in range(NT) for h in range(2)]
PIECES_2 = [(c, h, w) for c in range(NT)
            for h, w in ((0, (2 * (c % NJ) + c // NJ) // 2 + 1), (1, (2 * (c % NJ) + c // NJ + 1) // 2)) if w]
PIECES = {1: PIECES_1, 2: PIECES_2}

SIDES_1 = {
    0: [("f2.rs", -2)], 2: [("p1.tr", 1)], 5: [("p1.g1", 1)], 7: [("p1.g2", 1)], 8: [("f2.out", -2)],
    10: [("p1.w", 1), ("p1.h", 1)], 12: [("l2a", -2)], 19: [("p1.i", 1)], 22: [("l2b", -2)],
    23: [("p1.qa", 1), ("l2c", -2)], 25: [("p1.qb", 1), ("moe.tr", -2)], 26: [("p1.ka", 1)],
    27: [("moe.lg", -2)], 30: [("p1.kb", 1), ("r2", -1)],
}
SIDES_2 = {
    3: [("f1.rs", 0)], 5: [("f1.out", 0), ("l1a", 0)], 7: [("l1b", 0)], 15: [("l1c", 0)],
    19: [("p2.tr", 0)], 25: [("p2.qa", 0)], 28: [("p2.qb", 0), ("r1", 1)],
}
SIDES = {1: SIDES_1, 2: SIDES_2}
LATER = {
    "act": {"l1b": 8, "p1.h": 8, "p1.i": 3, "p1.kb": 3, "p2.qb": 6},
    "dve": {"l1b": 4, "l2a": 5, "p1.h": 1, "p1.kb": 4, "p1.tr": 1, "p2.qb": 8, "p2.tr": 3},
    "pool": {"l1a": 1, "l2a": 7, "p1.g2": 1},
}
PIECE_SLOTS = {
    1: [2, 2, 2, 4, 6, 11, 20, 20, 22, 23, 23, 24, 25, 26, 26],
    2: [2, 5, 5, 7, 9, 10, 14, 14, 14, 15, 19, 19, 19, 20, 23, 23],
}
VALUE_SLOTS = {1: [5, 14, 19, 22, 23, 24, 31, 2], 2: [9, 12, 12, 21, 22, 24, 28, 0]}
ADD_SLOTS = {1: [6, 10, 10, 20, 20, 24, 30, 6], 2: [5, 8, 18, 19, 19, 23, 26, 8]}
COPY_SLOT = {1: 0, 2: 0}
BIAS_SLOT = 9
STEPS = {
    "p1.tr": ["tr", "xt", "bn", "ag"], "p1.g1": ["mm", "gv", "d", "d2"],
    "p1.g2": ["mm", "ve", "rstd", "a", "ma", "b"], "p1.h": ["hf", "hh"], "p1.i": ["la", "lb", "hi"],
    "p1.qa": ["mm", "hi", "lo"], "p1.qb": ["mm", "hi", "lo"], "p1.ka": ["mm", "hi", "lo"],
    "p1.kb": ["mm", "hi", "lo", "k2"],
    "p2.tr": ["tr", "hh", "hi", "lo"], "p2.qa": ["mm", "hi", "lo"], "p2.qb": ["mm", "hi", "lo", "k2"],
    "p1.w": ["mm", "ws", "bb"],
    "f1.rs": ["mm", "tr", "ri"], "f1.out": ["mm", "sc", "t"],
    "f2.rs": ["mm", "tr", "ri"], "f2.out": ["mm", "sc", "t"],
    "moe.tr": ["tr", "ut"], "moe.lg": ["mm", "lg"],
    "r1": ["neg", "tr", "row"], "r2": ["neg", "tr", "row"],
    "e.top": ["max", "neg", "rest", "chosen"], "e.exp": [], "e.gate": ["recip", "gates"],
    "e.ta": ["tr", "copy"], "e.tb": ["tr", "copy"], "e.pool": ["mm", "copy"], "e.turn": ["tr", "copy"],
    "l1a": ["bn", "ag", "ve", "rs"], "l1b": ["nm", "va"], "l1c": ["v"],
    "l2a": ["bn", "ag", "ve", "rs"], "l2b": ["nm", "va"], "l2c": ["v"],
}
CHAIN = {"e.": "expert_step", "p1": "proj_step", "p2": "proj_step", "f1": "fin_step", "f2": "fin_step", "mo": "fin_step",
         "r1": "fin_step", "r2": "fin_step", "l1": "norm_step", "l2": "norm_step"}
LOOP_FIRST, LOOP_TRIPS = 2, 6
LAST = B
NG = B // BG
EXPERT_STEPS = ["e.top", "e.exp", "e.gate", "e.ta", "e.tb", "e.pool", "e.turn"]
EXPERT_SLOTS = {
    B - 1: {2 + 2 * k: [(EXPERT_STEPS[k % 7], k // 7)] for k in range(14)},
    B: {4 + 2 * k: [(name, 2)] for k, name in enumerate(EXPERT_STEPS)},
}
IN_MAIN = NG - 1


CHANNEL_CONSTS = {"wq": C, "wk": C, "wv_t": C, "wo": C, "a_wq": C, "a_wk": C, "a_wv_t": C, "gate_t": E,
                  "gn_scale": 1, "gn_bias": 1, "bq": 1, "bk": 1, "bv": 1}


def const_cols(name):
    names = list(CHANNEL_CONSTS)
    at = sum(CHANNEL_CONSTS[k] for k in names[:names.index(name)])
    return slice(at, at + CHANNEL_CONSTS[name])


PROLOGUE = ["p1.tr", "p1.g1", "p1.g2", "p1.w", "p1.h", "p1.i", "p1.qa", "p1.ka", "p1.kb", "p1.qb"]


def main_runs(ph, i):
    return i < B if ph == 1 else i >= 1


def pieces_image(ph, i):
    n = i - 1 if ph == 1 else i + 1
    return n, 0 <= n < B


class Image:

    def __init__(self, first, trip=None):
        self.first, self.trip = first, trip
        self.parity = first % 2

    def __add__(self, k):
        return Image(self.first + k, self.trip)

    @property
    def value(self):
        return self.first if self.trip is None else self.trip * 2 + self.first


def count_increments():
    counts, at = {}, {}

    def inc(sem, key, by=1):
        at[sem] = at.get(sem, 0) + by
        counts[sem, key] = at[sem]

    def side(name, n):
        for step in STEPS[name]:
            inc(CHAIN[name[:2]], (name, n, step))

    inc("x_loaded", ("x", 0), 16)
    inc("x_loaded", ("x", 1), 16)
    for name in PROLOGUE:
        side(name, 0)
    for p in range(len(PIECES_1)):
        inc("maxima_ready", (1, 0, p))
        inc("maxima_taken", (1, 0, p))
    side("r1", 0)
    for i in range(0, B + 1):
        for ph in (1, 2):
            n = i if ph == 1 else i - 1
            run = main_runs(ph, i)
            m, there = pieces_image(ph, i)
            if run:
                for u in range(len(UNITS[ph])):
                    inc("scores_ready", (ph, n, u))
                    inc("exp_done", (ph, n, u))
                for t in range(NT):
                    inc("values_done", (ph, n, t))
                    inc("rows_added", (ph, n, t))
                inc("out_copied", (ph, n))
                if ph == 1:
                    inc("bias_added", n)
            if there:
                for p in range(len(PIECES[3 - ph])):
                    inc("maxima_ready", (3 - ph, m, p))
                    inc("maxima_taken", (3 - ph, m, p))
            for slot in sorted(SIDES[ph]):
                for name, d in SIDES[ph][slot]:
                    if 0 <= i + d < B:
                        side(name, i + d)
            if ph == 1 and 0 <= i - 2:
                inc("block_stored", i - 2, 48)
            if ph == 1 and i + 2 < B:
                inc("x_loaded", ("x", i + 2), 16)
    for name in ("f2.rs", "f2.out", "l2a", "l2b", "l2c", "moe.tr", "moe.lg"):
        side(name, B - 1)
    for k in range(NG):
        for name in EXPERT_STEPS:
            side(name, k)
    inc("block_stored", B - 1, 48)
    return counts


COUNTS = count_increments()


def done(sem, *key):
    image = next((k for k in key if isinstance(k, Image)), None)
    flat = lambda n: tuple(n if isinstance(k, Image) else k for k in key)
    at = lambda n: COUNTS[sem, flat(n) if len(key) > 1 else n]
    if image is None:
        return COUNTS[sem, key if len(key) > 1 else key[0]]
    first = at(image.first)
    if image.trip is None:
        return first
    step = at(image.first + 2) - first
    for k in range(LOOP_TRIPS):
        assert at(image.first + 2 * k) == first + k * step, (sem, key)
    return image.trip * step + first


def earlier(sem, *key, back=1):
    v = done(sem, *key)
    image = next((k for k in key if isinstance(k, Image)), None)
    if isinstance(v, int) and v - back <= 0:
        return []
    return [v - back]


def exists(sem, *key):
    flat = tuple(k.first if isinstance(k, Image) else k for k in key)
    return (sem, flat if len(flat) > 1 else flat[0]) in COUNTS


def build_program(nc, x, out, by_channel, bo, gate_b, w1, w2, b2_t, shape_masks, block_rows):
    logits_dram = nc.dram_tensor("logits_scratch", (B, E, S), F32, kind="Internal").ap()
    t2_dram = nc.dram_tensor("t2_scratch", (B, S, C), F32, kind="Internal").ap()
    xv = x.rearrange("b (t p) c -> b p t c", p=P)
    t2v = t2_dram.rearrange("b (t p) c -> b p t c", p=P)
    out_pairs, t2_pairs = (ap.rearrange("b (j p a) c -> b p j (a c)", p=P, a=2) for ap in (out, t2_dram))
    whole = ExitStack()
    with whole:
        sb = lambda name, shape, dt=F32: whole.enter_context(nc.sbuf_tensor(name, shape, dt))
        u_all = sb("u_all", [P, B, NT * C])
        masks_f = sb("masks_f", [P, 4, P])
        ident_f = masks_f[:, 1, :]
        gate_b_sb = sb("gate_b_sb", [2 * E, 1])
        lg = sb("lg", [P, 2, S])
        rest = sb("rest", [P, S])
        top = sb("top", [P, NG, TOPK])
        stat = sb("stat", [P, NG, 3])
        gates = sb("gates", [P, NG, S])
        gates_t = sb("gates_t", [P, NT, P])
        pool_sb = sb("pool_sb", [P, C])
        pooled = sb("pooled", [C + 1, E, 32])
        logits_loaded = [whole.enter_context(nc.semaphore(f"logits_loaded{k}")) for k in range(NG)]
        expert_step = whole.enter_context(nc.semaphore("expert_step"))
        exp_ready = whole.enter_context(nc.semaphore("exp_ready"))
        with ExitStack() as ctx:
            attention_part(nc, ctx, locals())
        with ExitStack() as ctx:
            expert_part(nc, ctx, locals())


def choose_on_vector(nc, g, name, k):
    V, step, lg, rest, top, stat, gates = (nc.vector, *(g[n] for n in ("expert_step", "lg", "rest", "top", "stat", "gates")))

    def after(step_name):
        for v in earlier("expert_step", name, k, step_name):
            V.wait_ge(step, v)

    if name == "e.top":
        after("max")
        V.wait_ge(g["logits_loaded"][k], 16)
        V.max(top[:, k, :], lg[:, k % 2, :]).then_inc(step, 1)
        after("neg")
        V.tensor_scalar(stat[:, k, 0:1], top[:, k, 0:1], -1.0, None, ALU.mult).then_inc(step, 1)
        V.match_replace(rest[:, :], top[:, k, :], lg[:, k % 2, :], NEG_HUGE).then_inc(step, 1)
        after("chosen")
        V.tensor_tensor(rest[:, :], lg[:, k % 2, :], rest[:, :], ALU.not_equal).then_inc(step, 1)
    elif name == "e.gate":
        V.wait_ge(g["exp_ready"], k + 1)
        V.reciprocal(stat[:, k, 2:3], stat[:, k, 1:2]).then_inc(step, 1)
        after("gates")
        V.scalar_tensor_tensor(out=gates[:, k, :], in0=gates[:, k, :], scalar=stat[:, k, 2:3], in1=rest[:, :],
                               op0=ALU.mult, op1=ALU.mult).then_inc(step, 1)


def choose_on_scalar(nc, g, name, k, turn, pool_ps):
    step, gates, gates_t, pool_sb, pooled = (g[n] for n in ("expert_step", "gates", "gates_t", "pool_sb", "pooled"))
    if name == "e.exp":
        nc.scalar.wait_ge(step, done("expert_step", "e.top", k, "neg"))
        nc.scalar.activation(gates[:, k, :], g["lg"][:, k % 2, :], ACT.Exp, bias=g["stat"][:, k, 0:1], scale=1.0,
                             accum_out=g["stat"][:, k, 1:2]).then_inc(g["exp_ready"], 1)
    elif name in ("e.ta", "e.tb", "e.pool", "e.turn"):
        nc.scalar.wait_ge(step, done("expert_step", name, k, STEPS[name][0]))
        if name == "e.pool":
            ins = nc.scalar.copy(pool_sb[:, :], pool_ps[:, 0:C])
        elif name == "e.turn":
            ins = nc.scalar.copy(pooled[0:C, :, k * BG:(k + 1) * BG], pool_ps[0:C, P:2 * P].rearrange("c (b e) -> c e b", e=E))
        else:
            r = NJ * (name == "e.tb")
            ins = nc.scalar.copy(gates_t[:, r:r + NJ, :].rearrange("p t g -> p (t g)"), turn)
        ins.then_inc(step, 1)


def choose_on_tensor(nc, g, name, k, turn, pool_ps):
    pe, step, gates, gates_t, u_all, pool_sb, ident_f = (nc.tensor, *(
        g[n] for n in ("expert_step", "gates", "gates_t", "u_all", "pool_sb", "ident_f")))
    if name not in ("e.ta", "e.tb", "e.pool", "e.turn"):
        return
    pe.wait_ge(step, done("expert_step", name, k, STEPS[name][0]) - 1)
    if name == "e.pool":
        for t in range(NT):
            for b in range(BG):
                mm = pe.matmul(pool_ps[b * E:(b + 1) * E, 0:C], gates_t[:, t, b * E:(b + 1) * E],
                               u_all[:, k * BG + b, t * C:(t + 1) * C], start=t == 0, stop=t == NT - 1,
                               skip_group_check=True)
    elif name == "e.turn":
        mm = pe.transpose(pool_ps[0:C, P:2 * P], pool_sb[:, :], ident_f[:, :])
    else:
        r = NJ * (name == "e.tb")
        for t in range(NJ):
            mm = pe.transpose(turn[:, t * P:(t + 1) * P], gates[:, k, (r + t) * P:(r + t + 1) * P], ident_f[:, :])
    mm.then_inc(step, 1)


def attention_part(nc, ctx, g):
    (x, xv, logits_dram, t2v, u_all, masks_f, ident_f, gate_b_sb) = (
        g[k] for k in ("x", "xv", "logits_dram", "t2v", "u_all", "masks_f", "ident_f", "gate_b_sb"))

    def sb(name, shape, dt=F32):
        return ctx.enter_context(nc.sbuf_tensor(name, shape, dt))

    def ps(name, shape):
        return ctx.enter_context(nc.psum_tensor(name, shape, F32))

    def sem(name):
        return ctx.enter_context(nc.semaphore(name))

    scores = ps("scores", [P, NST, HALF])
    maxima_in = ps("maxima_in", [P, NM, HALF])
    values_out = ps("values_out", [P, HALF])
    proj_ps = ps("proj_ps", [P, HALF])
    fin_ps = ps("fin_ps", [P, HALF])

    keys = {s: [sb(f"keys{s}{q}", [P, S], F32R) for q in range(2)] for s in (1, 2)}
    keys_hi = {s: [sb(f"keys_hi{s}{q}", [KROWS, S], F32R) for q in range(2)] for s in (1, 2)}
    queries = {s: [sb(f"queries{s}{q}", [P, S], F32R) for q in range(2)] for s in (1, 2)}
    queries_lo = {s: [sb(f"queries_lo{s}{q}", [KROWS, S], F32R) for q in range(2)] for s in (1, 2)}
    probs = sb("probs", [P, NP, S])
    prob_sum = {s: sb(f"prob_sum{s}", [P, S]) for s in (1, 2)}
    maxima = {s: sb(f"maxima{s}", [P, NT, 2]) for s in (1, 2)}
    neg_max = {s: sb(f"neg_max{s}", [P, NT]) for s in (1, 2)}
    x_sb = [sb(f"x_sb{q}", [P, NT, C]) for q in range(2)]
    x_bias = sb("x_bias", [P, NT, C])
    t1 = [sb(f"t1{q}", [P, NT, C]) for q in range(2)]
    t2 = sb("t2", [P, NT, C])
    normed = [sb(f"normed{q}", [P, NT, C]) for q in range(2)]
    u_sb = sb("u_sb", [P, NT, C])
    ln_bn = sb("ln_bn", [P, NT, 6])
    ln_mv = sb("ln_mv", [P, NT, 2])
    ln = sb("ln", [P, 3, NT])
    xt = sb("xt", [P, HALF])
    h_full = sb("h_full", [P, HALF])
    h_hi = sb("h_hi", [P, HALF], F32R)
    h_stack = sb("h_stack", [P, S], F32R)
    bn = sb("bn", [P, 6])
    gn = sb("gn", [P, 12])
    affine = [sb(f"affine{q}", [P, 2]) for q in range(2)]
    out_raw = sb("out_raw", [P, HALF])
    row_sum = sb("row_sum", [P, NT, 32])
    recip = sb("recip", [P, NT])
    ut = sb("ut", [P, HALF])
    rows_mixed = sb("rows_mixed", [KROWS, S])
    logits = rows_mixed[0:E, :]
    block_rows = rows_mixed
    channel_consts = sb("channel_consts", [P, sum(CHANNEL_CONSTS.values())])
    const = lambda name, rows=slice(0, P): channel_consts[rows, const_cols(name)]
    m2_raw = sb("m2_raw", [P, P])
    w_hi = {k: sb(f"w_hi_{k}", [P, P], F32R) for k in ("q1", "k1", "m2")}
    w_lo = {k: sb(f"w_lo_{k}", [P, P], F32R) for k in ("q1", "k1", "m2")}
    w_out = {s: sb(f"w_out{s}", [P, P]) for s in (1, 2)}
    w_scaled = [sb(f"w_scaled{q}", [P, P]) for q in range(2)]
    bias_full = [sb(f"bias_full{q}", [P, C]) for q in range(2)]
    gate_bd = sb("gate_bd", [P, 2 * E])
    rows = sb("rows", [1, 2, C])
    bias_out = sb("bias_out", [P, C])
    ones_f = sb("ones_f", [P, P])
    minus_half = sb("minus_half", [P, NT])
    group_mean = masks_f[:, 0, :]
    ident_b = sb("ident_b", [P, P], BF16)
    mask_q = sb("mask_q", [P, P], BF16)
    mask_k = sb("mask_k", [P, P], BF16)

    names = ["x_loaded", "scores_ready", "exp_done", "values_done", "rows_added", "out_copied", "bias_added",
             "maxima_ready", "maxima_taken", "proj_step", "fin_step", "norm_step", "block_stored",
             "const_loaded", "zeroed", "const_step", "ones_set"]
    (x_loaded, scores_ready, exp_done, values_done, rows_added, out_copied, bias_added, maxima_ready,
     maxima_taken, proj_step, fin_step, norm_step, block_stored, const_loaded, zeroed, const_step,
     ones_set) = [
        sem(n) for n in names]
    block = ctx.enter_context(nc.Block())

    first, second = slice(0, C), slice(C, P)
    const_loads = [(masks_f[:, :, :], g["shape_masks"]), (channel_consts[first, :], g["by_channel"]),
                   (channel_consts[second, :], g["by_channel"]), (rows[:, 0, :], g["bo"]),
                   (block_rows[C:KROWS, :], g["block_rows"]), (gate_b_sb[0:E, :], g["gate_b"]),
                   (gate_b_sb[E:2 * E, :], g["gate_b"])]
    ALL_CONST = 16 * len(const_loads)

    def iterations(eng, emit):
        for k in range(LOOP_FIRST):
            emit(Image(k))
        with eng.Fori(0, LOOP_TRIPS) as trip:
            emit(Image(LOOP_FIRST, trip))
            emit(Image(LOOP_FIRST + 1, trip))
        for k in range(LOOP_FIRST + 2 * LOOP_TRIPS, LAST + 1):
            emit(Image(k))

    def sides(ph, i, slot, engine="pe"):
        later = LATER.get(engine, {})
        last = 2 * len(UNITS[ph]) - 1
        for at in range(slot + 1):
            for name, d in SIDES[ph].get(at, []):
                if min(at + later.get(name, 0), last) == slot and 0 <= i.first + d < B:
                    yield name, i + d

    def pieces(ph, i, slot):
        m, there = pieces_image(ph, i.first)
        if there:
            for p, at in enumerate(PIECE_SLOTS[ph]):
                if at == slot:
                    yield 3 - ph, i + (m - i.first), p

    def expert_sides(ph, i, slot):
        return EXPERT_SLOTS.get(i.first, {}).get(slot, []) if ph == 2 and i.trip is None else []

    def phase_before(ph, i):
        s, n = (2, i + (-2)) if ph == 1 else (1, i)
        return (s, n), 0 <= n.first < B

    def tiles(table, ph, i, slot):
        (s, m), there = phase_before(ph, i)
        if there and table[s][NT - 1] == slot:
            yield s, m, NT - 1
        for t in range(NT - 1):
            if main_runs(ph, i.first) and table[ph][t] == slot:
                yield ph, (i if ph == 1 else i + (-1)), t

    def cols(unit):
        t, a, j0 = unit
        return a * HALF + j0 * P, a * HALF + HALF

    def key_cols(t):
        c = (t % 2) * HALF + (t // 2) * P
        return slice(c, c + P)

    @block.sync
    def _(sp):
        sp.dma_start(x_sb[0][:, :, :], xv[0]).then_inc(x_loaded, 16)
        for dst, src in const_loads:
            sp.dma_start(dst, src).then_inc(const_loaded, 16)
        sp.dma_start(x_sb[1][:, :, :], xv[1]).then_inc(x_loaded, 16)

        def held(value):
            return value if isinstance(value, int) else sp.snap(value)

        def image_of(ap, at):
            return ap[at] if isinstance(at, int) else ap[bass.ds(at, 1)].squeeze(0)

        def load_logits(k):
            sp.wait_ge(block_stored, done("block_stored", (k + 1) * BG - 1))
            if k >= 2:
                sp.wait_ge(g["expert_step"], done("expert_step", "e.top", k - 2, "chosen"))
                sp.wait_ge(g["exp_ready"], k - 1)
            sp.dma_start(g["lg"][:, k % 2, :], logits_dram[k * BG:(k + 1) * BG].rearrange("b e s -> (b e) s")).then_inc(
                g["logits_loaded"][k], 16)

        def emit(i):
            for k in range(IN_MAIN):
                if i.trip is None and (i.first == B - 1 and k < 2 or i.first == B and k == 2):
                    load_logits(k)
            if i.first >= 2:
                store(i + (-2))
            if i.first + 2 < B:
                at = held((i + 2).value)
                sp.wait_ge(fin_step, done("fin_step", "f1.out", i, "t"))
                sp.dma_start(x_sb[i.parity][:, :, :], image_of(xv, at)).then_inc(x_loaded, 16)

        def store(n):
            at, normed_u, logits_there = (held(n.value), held(done("norm_step", "l2c", n, "v")),
                                          held(done("fin_step", "moe.lg", n, "lg")))
            sp.wait_ge(norm_step, normed_u)
            u_dst = u_all[:, n.value, :] if n.trip is None else u_all[:, bass.ds(at, 1), :].squeeze(1)
            sp.dma_start(u_dst, u_sb[:, :, :].rearrange("p t c -> p (t c)")).then_inc(block_stored, 16)
            sp.dma_start(image_of(t2v, at), t2[:, :, :]).then_inc(block_stored, 16)
            sp.wait_ge(fin_step, logits_there)
            sp.dma_start(image_of(logits_dram, at), logits).then_inc(block_stored, 16)

        iterations(sp, emit)
        store(Image(B - 1))
        sp.wait_ge(block_stored, 48 * B)

    @block.tensor
    def _(pe):
        def transposes(dst, src):
            for j in range(NJ):
                mm = pe.transpose(dst[:, j * P:(j + 1) * P],
                                  src[:, 2 * j:2 * j + 2, :].rearrange("p t c -> p (t c)"), ident_f[:, :])
            return mm

        def project(w, src, a):
            pe.matmul(proj_ps[:, :], w_lo[w][:, :], src[:, a * HALF:(a + 1) * HALF], start=True, stop=False)
            return pe.matmul(proj_ps[:, :], w_hi[w][:, :], src[:, a * HALF:(a + 1) * HALF], start=False, stop=True)

        def side(name, n):
            q = n.parity
            first = STEPS[name][0]
            if name[:2] in ("p1", "p2"):
                for v in earlier("proj_step", name, n, "tr" if name.endswith("tr") else "mm") if name not in ("p1.h", "p1.i") else []:
                    pe.wait_ge(proj_step, v)
                if name == "p1.tr":
                    pe.wait_ge(x_loaded, done("x_loaded", "x", n))
                    transposes(proj_ps, x_sb[q]).then_inc(proj_step, 1)
                elif name == "p1.g1":
                    pe.matmul(proj_ps[:, 0:2], group_mean[:, :], gn[:, 0:2], start=True, stop=True).then_inc(proj_step, 1)
                elif name == "p1.g2":
                    pe.matmul(proj_ps[:, 0:2], group_mean[:, :], gn[:, 4:6], start=True, stop=True).then_inc(proj_step, 1)
                elif name == "p1.w":
                    pe.matmul(proj_ps[:, 0:C], affine[q][0:C, 1:2].to_broadcast([C, P]), w_out[1][0:C, 0:C],
                              start=True, stop=True).then_inc(proj_step, 1)
                elif name in ("p1.qa", "p1.qb"):
                    project("q1", h_stack, int(name == "p1.qb")).then_inc(proj_step, 1)
                elif name in ("p1.ka", "p1.kb"):
                    project("k1", h_stack, int(name == "p1.kb")).then_inc(proj_step, 1)
                elif name == "p2.tr":
                    pe.wait_ge(norm_step, done("norm_step", "l1c", n, "v"))
                    transposes(proj_ps, normed[q]).then_inc(proj_step, 1)
                elif name in ("p2.qa", "p2.qb"):
                    project("m2", keys[2][q], int(name == "p2.qb")).then_inc(proj_step, 1)
            elif name in ("f1.rs", "f2.rs"):
                s = int(name[1])
                for v in earlier("fin_step", name, n, "mm"):
                    pe.wait_ge(fin_step, v)
                pe.wait_ge(rows_added, done("rows_added", s, n, NT - 1))
                for r in range(4):
                    mm = pe.matmul(fin_ps[r * 32:(r + 1) * 32, 0:NT * 32], ones_f[:, 0:32],
                                   prob_sum[s][:, :].rearrange("p (k q) -> p k q", q=P)[:, :, r * 32:(r + 1) * 32],
                                   start=True, stop=True)
                mm.then_inc(fin_step, 1)
            elif name in ("f1.out", "f2.out"):
                s = int(name[1])
                for v in earlier("fin_step", name, n, "mm"):
                    pe.wait_ge(fin_step, v)
                pe.wait_ge(out_copied, done("out_copied", s, n))
                if s == 1:
                    pe.wait_ge(proj_step, done("proj_step", "p1.w", n, "ws"))
                weights = w_scaled[q] if s == 1 else w_out[2]
                for j in range(NJ):
                    mm = pe.matmul(fin_ps[:, j * P:(j + 1) * P], out_raw[:, j * P:(j + 1) * P], weights[:, :],
                                   start=True, stop=True)
                mm.then_inc(fin_step, 1)
            elif name == "moe.tr":
                for v in earlier("fin_step", name, n, "tr"):
                    pe.wait_ge(fin_step, v)
                pe.wait_ge(norm_step, done("norm_step", "l2c", n, "v"))
                transposes(fin_ps, u_sb).then_inc(fin_step, 1)
            elif name == "moe.lg":
                for v in earlier("fin_step", name, n, "mm"):
                    pe.wait_ge(fin_step, v)
                pe.matmul(fin_ps[0:2 * E, :], gate_bd[:, :], ut[:, :], start=True, stop=True).then_inc(fin_step, 1)
            elif name in ("r1", "r2"):
                s = int(name[1])
                for v in earlier("fin_step", name, n, "tr"):
                    pe.wait_ge(fin_step, v)
                pe.matmul(fin_ps[C:KROWS, 0:P], neg_max[s][:, :], ident_f[:, :], start=True, stop=True).then_inc(fin_step, 1)

        def piece(s, n, p):
            c, h, w = PIECES[s][p]
            q = n.parity
            if (s, n.first, p) == (2, B - 1, 0) and n.trip is None:
                pe.wait_ge(g["expert_step"], done("expert_step", "e.turn", 1, "copy"))
            if (s, n.first, p) == (1, 0, len(PIECES_1) // 2) and n.trip is None:
                pe.wait_ge(proj_step, done("proj_step", PROLOGUE[-1], n, "lo"))
            if p == 0:
                pe.wait_ge(proj_step, done("proj_step", "p1.kb" if s == 1 else "p2.qb", n, "k2"))
            for v in earlier("maxima_taken", s, n, p, back=min(p + 1, NM)):
                pe.wait_ge(maxima_taken, v)
            t = 2 * (c % NJ) + c // NJ
            diagonal = s == 2 and h == t % 2
            if diagonal:
                pe.matmul(maxima_in[:, p % NM, (w - 1) * P:w * P], ident_b[:, :], mask_q[:, :], start=True, stop=True)
            pe.matmul(maxima_in[:, p % NM, 0:w * P], queries[s][q][:, c * P:(c + 1) * P],
                      keys[s][q][:, h * HALF:h * HALF + w * P], start=not diagonal, stop=True,
                      skip_group_check=diagonal).then_inc(maxima_ready, 1)

        def score(s, n, u):
            t, a, j0 = UNITS[s][u]
            q = n.parity
            lo, hi = cols(UNITS[s][u])
            if u == 0:
                pe.wait_ge(fin_step, done("fin_step", f"r{s}", n, "row"))
            for v in earlier("exp_done", s, n, u, back=1 if (s, u) == (1, 0) else NST):
                pe.wait_ge(exp_done, v)
            bank = scores[:, (u + (s - 1) * len(UNITS_1)) % NST, 0:hi - lo]
            diagonal = s == 2 and a == t % 2
            if diagonal:
                pe.matmul(bank[:, 0:P], ident_b[:, :], mask_k[:, :], start=True, stop=True)
            pe.matmul(bank, keys_hi[s][q][:, key_cols(t)], queries_lo[s][q][:, lo:hi], start=not diagonal, stop=False,
                      skip_group_check=diagonal)
            pe.matmul(bank, keys[s][q][:, key_cols(t)], queries[s][q][:, lo:hi], start=False, stop=True,
                      skip_group_check=diagonal).then_inc(scores_ready, 1)

        def values(s, n, t):
            v_sb = x_sb[n.parity] if s == 1 else normed[n.parity]
            us = [u for u, unit in enumerate(UNITS[s]) if unit[0] == t]
            if t == 0:
                for v in earlier("out_copied", s, n):
                    pe.wait_ge(out_copied, v)
            pe.wait_ge(exp_done, done("exp_done", s, n, us[-1]))
            for u in us:
                _, a, j0 = UNITS[s][u]
                lo, hi = cols(UNITS[s][u])
                mm = pe.matmul(values_out[a * C:(a + 1) * C, j0 * P:HALF], v_sb[:, t, :], probs[:, t % NP, lo:hi],
                               start=t == 0, stop=t == NT - 1, skip_group_check=True)
            mm.then_inc(values_done, 1)

        pe.wait_ge(const_loaded, ALL_CONST)
        pe.wait_ge(const_step, 1)
        pe.matmul(fin_ps[0:C, 0:C], const("wv_t", first), const("wo", first), start=True, stop=True)
        pe.matmul(fin_ps[0:1, C:2 * C], const("bv", first), const("wo", first), start=True, stop=True)
        for r in (first, second):
            mm = pe.matmul(fin_ps[r, 2 * C:3 * C], const("a_wq", first), const("a_wk", first), start=True, stop=True)
        mm.then_inc(const_step, 1)
        pe.wait_ge(const_step, 4)
        pe.matmul(fin_ps[:, 0:C], ones_f[0:1, :], rows[:, 1, :], start=True, stop=True).then_inc(const_step, 1)
        pe.wait_ge(const_step, 6)
        pe.wait_ge(zeroed, 4)

        for name in PROLOGUE:
            side(name, Image(0))
        for p in range(len(PIECES_1)):
            piece(1, Image(0), p)
        side("r1", Image(0))

        def extras(ph, i, slot):
            for s, m, p in pieces(ph, i, slot):
                piece(s, m, p)
            for name, m in sides(ph, i, slot):
                side(name, m)
            for name, k in expert_sides(ph, i, slot):
                if (name, k) == ("e.ta", 0):
                    pe.wait_ge(maxima_taken, done("maxima_taken", 1, B - 1, len(PIECES_1) - 1))
                if (name, k) == ("e.ta", 2):
                    pe.wait_ge(maxima_taken, done("maxima_taken", 2, B - 1, len(PIECES_2) - 1))
                if name == "e.pool":
                    pe.wait_ge(block_stored, done("block_stored", (k + 1) * BG - 1))
                choose_on_tensor(nc, g, name, k, maxima_in[:, 0, :], maxima_in[:, 1, :])

        def emit(i):
            for ph in (1, 2):
                n = i if ph == 1 else i + (-1)
                for slot in range(2 * len(UNITS[ph])):
                    if slot % 2 == 0 and main_runs(ph, i.first):
                        score(ph, n, slot // 2)
                    for s, m, t in tiles(VALUE_SLOTS, ph, i, slot):
                        values(s, m, t)
                    extras(ph, i, slot)

        pe.wait_ge(ones_set, 1)
        iterations(pe, emit)
        values(2, Image(B - 1), NT - 1)
        for name in ("f2.rs", "f2.out", "moe.tr", "moe.lg"):
            side(name, Image(B - 1))

    @block.scalar
    def _(act):
        def round_to(dst, src, bias=0.0):
            return nc.scalar.activation(dst, src, ACT.Identity, bias=bias, scale=1.0)

        def side(name, n):
            q = n.parity
            if name == "p1.tr":
                act.wait_ge(proj_step, done("proj_step", name, n, "tr"))
                nc.scalar.copy(xt[:, :], proj_ps[:, :]).then_inc(proj_step, 1)
            elif name == "p1.h":
                act.wait_ge(proj_step, done("proj_step", name, n, "hf"))
                nc.scalar.copy(h_hi[:, :], h_full[:, :]).then_inc(proj_step, 1)
            elif name == "p1.i":
                act.wait_ge(proj_step, done("proj_step", name, n, "lb"))
                nc.scalar.copy(h_stack[0:C, 0:HALF], h_hi[0:C, :])
                nc.scalar.copy(h_stack[0:C, HALF:S], h_hi[C:P, :]).then_inc(proj_step, 1)
            elif name in ("p1.qa", "p1.qb", "p1.ka", "p1.kb"):
                a = int(name[-1] == "b")
                act.wait_ge(proj_step, done("proj_step", name, n, "mm"))
                dst, b = (queries[1][q], "bq") if name[3] == "q" else (keys[1][q], "bk")
                round_to(dst[:, a * HALF:(a + 1) * HALF], proj_ps[:, :], const(b)).then_inc(proj_step, 1)
                if name == "p1.kb":
                    act.wait_ge(proj_step, done("proj_step", name, n, "lo"))
                    nc.scalar.copy(keys_hi[1][q][0:C, :], keys[1][q][0:C, :]).then_inc(proj_step, 1)
            elif name == "p2.tr":
                act.wait_ge(proj_step, done("proj_step", name, n, "tr"))
                nc.scalar.copy(h_hi[:, :], proj_ps[:, :]).then_inc(proj_step, 1)
                nc.scalar.copy(keys[2][q][0:C, 0:HALF], proj_ps[0:C, :])
                nc.scalar.copy(keys[2][q][0:C, HALF:S], proj_ps[C:P, :]).then_inc(proj_step, 1)
            elif name in ("p2.qa", "p2.qb"):
                a = int(name[-1] == "b")
                act.wait_ge(proj_step, done("proj_step", name, n, "mm"))
                nc.scalar.copy(queries[2][q][:, a * HALF:(a + 1) * HALF], proj_ps[:, :]).then_inc(proj_step, 1)
                if name == "p2.qb":
                    act.wait_ge(proj_step, done("proj_step", name, n, "lo"))
                    nc.scalar.copy(keys_hi[2][q][0:C, :], keys[2][q][0:C, :]).then_inc(proj_step, 1)
            elif name in ("l1b", "l2b", "l1c", "l2c"):
                src, dst = (t1[q], normed[q]) if name[1] == "1" else (t2, u_sb)
                if name == "l1b" and exists("values_done", 2, n + (-2), NT - 1):
                    act.wait_ge(values_done, done("values_done", 2, n + (-2), NT - 1))
                if name == "l2b" and exists("block_stored", n + (-1)):
                    act.wait_ge(block_stored, done("block_stored", n + (-1)))
                if name[2] == "b":
                    act.wait_ge(norm_step, done("norm_step", name, n, "nm"))
                for t in range(NT)[:NJ] if name[2] == "b" else range(NT)[NJ:]:
                    ins = nc.scalar.activation(dst[:, t, :], src[:, t, :], ACT.Identity, bias=ln[:, 2, t:t + 1],
                                               scale=ln[:, 1, t:t + 1])
                ins.then_inc(norm_step, 1)
            elif name == "moe.tr":
                act.wait_ge(fin_step, done("fin_step", name, n, "tr"))
                nc.scalar.copy(ut[:, :], fin_ps[:, :]).then_inc(fin_step, 1)
            elif name == "moe.lg":
                act.wait_ge(fin_step, done("fin_step", name, n, "mm"))
                if exists("block_stored", n + (-1)):
                    act.wait_ge(block_stored, done("block_stored", n + (-1)))
                for a in range(2):
                    mm = nc.scalar.activation(
                        logits.rearrange("e (j a t) -> e j a t", a=2, t=P)[:, :, a, :],
                        fin_ps[a * E:(a + 1) * E, :].rearrange("e (j t) -> e j t", t=P), ACT.Identity,
                        bias=gate_b_sb[a * E:(a + 1) * E, :], scale=1.0)
                mm.then_inc(fin_step, 1)

        def exponentials(s, n, u):
            t, a, j0 = UNITS[s][u]
            lo, hi = cols(UNITS[s][u])
            if u == 0 or UNITS[s][u - 1][0] != t:
                for v in earlier("values_done", s, n, t, back=NP):
                    act.wait_ge(values_done, v)
                for v in earlier("rows_added", s, n, t, back=NP):
                    act.wait_ge(rows_added, v)
            act.wait_ge(scores_ready, done("scores_ready", s, n, u))
            nc.scalar.activation(probs[:, t % NP, lo:hi], scores[:, (u + (s - 1) * len(UNITS_1)) % NST, 0:hi - lo], ACT.Exp,
                                 scale=SCALE).then_inc(exp_done, 1)

        def copy_out(s, n):
            act.wait_ge(values_done, done("values_done", s, n, NT - 1))
            other = ("f2.out", n + (-2)) if s == 1 else ("f1.out", n + 1)
            if exists("fin_step", other[0], other[1], "mm"):
                act.wait_ge(fin_step, done("fin_step", other[0], other[1], "mm"))
            nc.scalar.copy(out_raw[:, :], values_out[:, :]).then_inc(out_copied, 1)

        act.wait_ge(const_step, 2)
        nc.scalar.copy(w_out[1][0:C, 0:C], fin_ps[0:C, 0:C])
        nc.scalar.copy(w_out[1][C:P, C:P], fin_ps[0:C, 0:C])
        for c in (first, second):
            nc.scalar.copy(m2_raw[:, c], fin_ps[:, 2 * C:3 * C])
        nc.scalar.activation(rows[:, 1, :], fin_ps[0:1, C:2 * C], ACT.Copy).then_inc(const_step, 1)
        act.wait_ge(const_step, 5)
        nc.scalar.copy(bias_out[:, :], fin_ps[:, 0:C]).then_inc(const_step, 1)
        act.wait_ge(const_loaded, ALL_CONST)

        for name in PROLOGUE:
            side(name, Image(0))

        def emit(i):
            for ph in (1, 2):
                n = i if ph == 1 else i + (-1)
                for slot in range(2 * len(UNITS[ph])):
                    if slot % 2 == 0 and main_runs(ph, i.first):
                        exponentials(ph, n, slot // 2)
                    before, there = phase_before(ph, i)
                    if there and slot == COPY_SLOT[before[0]]:
                        copy_out(*before)
                    for name, m in sides(ph, i, slot, "act"):
                        side(name, m)
                    for name, k in expert_sides(ph, i, slot):
                        choose_on_scalar(nc, g, name, k, maxima_in[:, 0, :], maxima_in[:, 1, :])

        act.wait_ge(ones_set, 1)
        iterations(act, emit)
        copy_out(2, Image(B - 1))
        for name in ("f2.rs", "f2.out", "l2a", "l2b", "l2c", "moe.tr", "moe.lg"):
            side(name, Image(B - 1))

    @block.gpsimd
    def _(pool):
        def side(name, n):
            if name == "p1.g2":
                pool.wait_ge(proj_step, done("proj_step", name, n, "ve"))
                nc.gpsimd.tensor_tensor(gn[:, 7:8], gn[:, 6:7], minus_half[:, 0:1], ALU.pow).then_inc(proj_step, 1)
            elif name in ("l1a", "l2a"):
                pool.wait_ge(norm_step, done("norm_step", name, n, "ve"))
                nc.gpsimd.tensor_tensor(ln[:, 1, :], ln[:, 0, :], minus_half[:, :], ALU.pow).then_inc(norm_step, 1)

        def add_rows(s, n, t):
            us = [u for u, unit in enumerate(UNITS[s]) if unit[0] == t]
            total, new = prob_sum[s], probs[:, t % NP, :]
            if t == 0:
                return
            pool.wait_ge(exp_done, done("exp_done", s, n, us[-1]))
            if t == 1:
                if exists("fin_step", f"f{s}.rs", n + (-1), "mm"):
                    pool.wait_ge(fin_step, done("fin_step", f"f{s}.rs", n + (-1), "mm"))
                lo = 0 if s == 1 else P
                if lo:
                    nc.gpsimd.tensor_tensor(total[:, 0:lo], probs[:, 0, 0:lo], ones_f[:, 0:lo], ALU.mult)
                nc.gpsimd.tensor_tensor(total[:, lo:], probs[:, 0, lo:], new[:, lo:], ALU.add).then_inc(rows_added, 2)
                return
            pool.wait_ge(rows_added, done("rows_added", s, n, t - 1))
            los = [cols(UNITS[s][u]) for u in us]
            if len(los) == 2 and los[0][0] + HALF == los[1][0]:
                w = HALF - los[0][0]
                view = lambda ap: ap.rearrange("p (a c) -> p a c", a=2)[:, :, HALF - w:HALF]
                nc.gpsimd.tensor_tensor(view(total[:, :]), view(total[:, :]), view(new), ALU.add).then_inc(rows_added, 1)
            else:
                for lo, hi in los:
                    ins = nc.gpsimd.tensor_tensor(total[:, lo:hi], total[:, lo:hi], new[:, lo:hi], ALU.add)
                ins.then_inc(rows_added, 1)

        def add_bias(n):
            pool.wait_ge(proj_step, done("proj_step", "p1.w", n, "bb"))
            if exists("fin_step", "f1.out", n + (-1), "t"):
                pool.wait_ge(fin_step, done("fin_step", "f1.out", n + (-1), "t"))
            nc.gpsimd.tensor_tensor(x_bias[:, :, :], x_sb[n.parity][:, :, :],
                                    bias_full[n.parity][:, :].unsqueeze(1).to_broadcast([P, NT, C]), ALU.add).then_inc(bias_added, 1)

        nc.gpsimd.memset(minus_half[:, :], -0.5)
        nc.gpsimd.memset(ones_f[:, :], 1.0).then_inc(zeroed, 1)
        pool.wait_ge(zeroed, 1)
        pool.wait_ge(const_step, 6)
        for name in PROLOGUE:
            side(name, Image(0))

        def emit(i):
            for ph in (1, 2):
                for slot in range(2 * len(UNITS[ph])):
                    for s, m, t in tiles(ADD_SLOTS, ph, i, slot):
                        add_rows(s, m, t)
                    if ph == 1 and main_runs(ph, i.first) and slot == BIAS_SLOT:
                        add_bias(i)
                    for name, m in sides(ph, i, slot, "pool"):
                        side(name, m)

        iterations(pool, emit)
        add_rows(2, Image(B - 1), NT - 1)
        side("l2a", Image(B - 1))

    @block.vector
    def _(dve):
        V = nc.vector

        def side(name, n):
            q = n.parity

            def step(chain, sem_, step_name):
                for v in earlier(chain, name, n, step_name):
                    dve.wait_ge(sem_, v)

            if name == "p1.tr":
                step("proj_step", proj_step, "bn")
                V.bn_stats(bn[:, :], xt[:, :]).then_inc(proj_step, 1)
                step("proj_step", proj_step, "ag")
                V.memset(gn[:, 11:12], 0.0)
                V.bn_aggr(gn[:, 0:2], bn[:, :]).then_inc(proj_step, 1)
            elif name == "p1.g1":
                step("proj_step", proj_step, "gv")
                V.tensor_copy(gn[:, 2:4], proj_ps[:, 0:2]).then_inc(proj_step, 1)
                step("proj_step", proj_step, "d")
                V.tensor_scalar(gn[:, 4:6], gn[:, 0:2], gn[:, 2:3], None, ALU.subtract).then_inc(proj_step, 1)
                step("proj_step", proj_step, "d2")
                V.tensor_tensor(gn[:, 4:6], gn[:, 4:6], gn[:, 4:6], ALU.mult).then_inc(proj_step, 1)
            elif name == "p1.g2":
                step("proj_step", proj_step, "ve")
                V.scalar_tensor_tensor(out=gn[:, 6:7], in0=proj_ps[:, 0:1], scalar=EPS_GN, in1=gn[:, 3:4],
                                       op0=ALU.add, op1=ALU.add).then_inc(proj_step, 1)
                step("proj_step", proj_step, "a")
                V.tensor_tensor(affine[q][:, 0:1], gn[:, 7:8], const("gn_scale"), ALU.mult).then_inc(proj_step, 1)
                step("proj_step", proj_step, "ma")
                V.tensor_tensor(gn[:, 8:9], gn[:, 2:3], affine[q][:, 0:1], ALU.mult).then_inc(proj_step, 1)
                step("proj_step", proj_step, "b")
                V.tensor_tensor(affine[q][:, 1:2], const("gn_bias"), gn[:, 8:9], ALU.subtract).then_inc(proj_step, 1)
            elif name == "p1.w":
                step("proj_step", proj_step, "ws")
                V.tensor_scalar(w_scaled[q][:, :], w_out[1][:, :], affine[q][:, 0:1], None, ALU.mult).then_inc(proj_step, 1)
                if exists("bias_added", n + (-2)):
                    dve.wait_ge(bias_added, done("bias_added", n + (-2)))
                V.tensor_tensor(bias_full[q][:, :], proj_ps[:, 0:C], bias_out[:, :], ALU.add).then_inc(proj_step, 1)
            elif name == "p1.h":
                step("proj_step", proj_step, "hf")
                V.tensor_scalar(h_full[:, :], xt[:, :], affine[q][:, 0:1], affine[q][:, 1:2], ALU.mult,
                                ALU.add).then_inc(proj_step, 1)
            elif name == "p1.i":
                step("proj_step", proj_step, "la")
                V.tensor_tensor(h_stack[C:P, 0:HALF], h_full[0:C, :], h_hi[0:C, :], ALU.subtract).then_inc(proj_step, 1)
                V.tensor_tensor(h_stack[C:P, HALF:S], h_full[C:P, :], h_hi[C:P, :], ALU.subtract).then_inc(proj_step, 1)
            elif name in ("p1.qa", "p1.qb"):
                c = slice(HALF * (name[-1] == "b"), HALF * (name[-1] == "b") + HALF)
                step("proj_step", proj_step, "lo")
                V.scalar_tensor_tensor(out=queries_lo[1][q][0:C, c], in0=proj_ps[0:C, :], scalar=const("bq", first),
                                       in1=queries[1][q][0:C, c], op0=ALU.add, op1=ALU.subtract).then_inc(proj_step, 1)
            elif name in ("p1.ka", "p1.kb"):
                c = slice(HALF * (name[-1] == "b"), HALF * (name[-1] == "b") + HALF)
                step("proj_step", proj_step, "lo")
                V.scalar_tensor_tensor(out=keys[1][q][C:P, c], in0=proj_ps[C:P, :], scalar=const("bk", second),
                                       in1=keys[1][q][C:P, c], op0=ALU.add, op1=ALU.subtract).then_inc(proj_step, 1)
            elif name == "p2.tr":
                step("proj_step", proj_step, "lo")
                V.tensor_tensor(keys[2][q][C:P, 0:HALF], proj_ps[0:C, :], h_hi[0:C, :], ALU.subtract)
                V.tensor_tensor(keys[2][q][C:P, HALF:S], proj_ps[C:P, :], h_hi[C:P, :], ALU.subtract).then_inc(proj_step, 1)
            elif name in ("p2.qa", "p2.qb"):
                c = slice(HALF * (name[-1] == "b"), HALF * (name[-1] == "b") + HALF)
                step("proj_step", proj_step, "lo")
                V.tensor_tensor(queries_lo[2][q][0:C, c], proj_ps[0:C, :], queries[2][q][0:C, c],
                                ALU.subtract).then_inc(proj_step, 1)
            elif name in ("f1.rs", "f2.rs"):
                s = int(name[1])
                step("fin_step", fin_step, "tr")
                V.transpose(row_sum[:, :, :].rearrange("p k q -> p (k q)"), fin_ps[:, 0:NT * 32]).then_inc(fin_step, 1)
                step("fin_step", fin_step, "ri")
                V.reciprocal(recip[:, :].rearrange("p (j a) -> p a j", a=2),
                             row_sum[:, :, 0].rearrange("p (a j) -> p a j", a=2)).then_inc(fin_step, 1)
            elif name in ("f1.out", "f2.out"):
                if name == "f2.out" and exists("block_stored", n + (-1)):
                    dve.wait_ge(block_stored, done("block_stored", n + (-1)))
                step("fin_step", fin_step, "sc")
                dst, base = (t1[q], x_bias) if name == "f1.out" else (t2, t1[q])
                V.tensor_tensor(dst[:, :, :], fin_ps[:, :].rearrange("p (t c) -> p t c", c=C),
                                recip[:, :].unsqueeze(2).to_broadcast([P, NT, C]), ALU.mult).then_inc(fin_step, 1)
                if name == "f1.out":
                    dve.wait_ge(bias_added, done("bias_added", n))
                step("fin_step", fin_step, "t")
                V.tensor_tensor(dst[:, :, :], dst[:, :, :], base[:, :, :], ALU.add).then_inc(fin_step, 1)
            elif name in ("l1a", "l2a"):
                src = t1[q] if name == "l1a" else t2
                dve.wait_ge(fin_step, done("fin_step", f"f{name[1]}.out", n, "t"))
                step("norm_step", norm_step, "bn")
                for t in range(NT):
                    ins = V.bn_stats(ln_bn[:, t, :], src[:, t, :])
                ins.then_inc(norm_step, 1)
                step("norm_step", norm_step, "ag")
                V.memset(ln[:, 2, :], 0.0)
                for t in range(NT):
                    ins = V.bn_aggr(ln_mv[:, t, :], ln_bn[:, t, :])
                ins.then_inc(norm_step, 1)
                step("norm_step", norm_step, "ve")
                V.tensor_scalar(ln[:, 0, :], ln_mv[:, :, 1], EPS_LN, None, ALU.add).then_inc(norm_step, 1)
            elif name in ("l1b", "l2b"):
                step("norm_step", norm_step, "nm")
                V.scalar_tensor_tensor(out=ln[:, 2, :], in0=ln_mv[:, :, 0], scalar=-1.0, in1=ln[:, 1, :],
                                       op0=ALU.mult, op1=ALU.mult).then_inc(norm_step, 1)
            elif name in ("r1", "r2"):
                s = int(name[1])
                dve.wait_ge(maxima_taken, done("maxima_taken", s, n, len(PIECES[s]) - 1))
                step("fin_step", fin_step, "neg")
                V.tensor_reduce(neg_max[s][:, :], maxima[s][:, :, :], AX.X, ALU.max, negate=True).then_inc(fin_step, 1)
                step("fin_step", fin_step, "row")
                V.tensor_tensor(
                    queries_lo[s][q][C:KROWS, :].rearrange("r (c t) -> r c t", t=P),
                    fin_ps[C:KROWS, 0:P].unsqueeze(1).to_broadcast([NT, NT, P]),
                    block_rows[C:KROWS, :].rearrange("r (c t) -> r c t", t=P), ALU.mult).then_inc(fin_step, 1)

        def piece(s, n, p):
            c, h, w = PIECES[s][p]
            dve.wait_ge(maxima_ready, done("maxima_ready", s, n, p))
            V.reduce_max(maxima[s][:, c, h:h + 1], maxima_in[:, p % NM, 0:w * P], AX.X).then_inc(maxima_taken, 1)

        V.memset(w_out[1][:, :], 0.0)
        V.memset(w_out[2][:, :], 0.0)
        V.memset(gate_bd[:, :], 0.0)
        V.memset(maxima[2][:, :, :], NEG_HUGE).then_inc(zeroed, 1)
        dve.wait_ge(zeroed, 2)
        dve.wait_ge(const_loaded, ALL_CONST)
        V.tensor_copy(ident_b[:, :], ident_f[:, :])
        for h, r in enumerate((first, second)):
            V.tensor_copy(w_out[2][r, r], const("a_wv_t", r))
            V.tensor_copy(gate_bd[r, h * E:(h + 1) * E], const("gate_t", r))
        V.tensor_copy(mask_q[:, :], masks_f[:, 2, :])
        V.tensor_copy(mask_k[:, :], masks_f[:, 3, :]).then_inc(const_step, 1)
        dve.wait_ge(const_step, 3)
        V.tensor_tensor(rows[:, 1, :], rows[:, 1, :], rows[:, 0, :], ALU.add).then_inc(const_step, 1)
        twice = lambda name: const(name).unsqueeze(1).to_broadcast([P, 2, C])
        raw = {"q1": twice("wq"), "k1": twice("wk"), "m2": m2_raw[:, :].rearrange("p (r c) -> p r c", c=C)}
        blocks = lambda w: w[:, :].rearrange("p (r c) -> p r c", c=C)
        for k in raw:
            ins = V.tensor_copy(blocks(w_hi[k]), raw[k])
        ins.then_inc(zeroed, 1)
        dve.wait_ge(zeroed, 3)
        for k in raw:
            ins = V.tensor_tensor(blocks(w_lo[k]), raw[k], blocks(w_hi[k]), ALU.subtract)
        ins.then_inc(zeroed, 1)

        fills = {"p1.g1": (g["pooled"][0:C, :, :], 0.0), "p1.w": (g["pooled"][C:C + 1, :, :], 1.0)}
        for name, s, q in (("p1.h", 1, 0), ("p1.i", 1, 1), ("p1.qa", 2, 0), ("p1.ka", 2, 1)):
            fills[name] = (keys_hi[s][q][C:KROWS, :].bitcast(F32), 1.0)
        for name in PROLOGUE[:-1]:
            side(name, Image(0))
            if name in fills:
                ins = V.memset(*fills[name])
                if name == "p1.ka":
                    ins.then_inc(ones_set, 1)
        for p in range(len(PIECES_1)):
            piece(1, Image(0), p)
            if p == 1:
                side(PROLOGUE[-1], Image(0))
        side("r1", Image(0))

        def emit(i):
            for ph in (1, 2):
                for slot in range(2 * len(UNITS[ph])):
                    for s, m, p in pieces(ph, i, slot):
                        piece(s, m, p)
                    for name, m in sides(ph, i, slot, "dve"):
                        side(name, m)
                    for name, k in expert_sides(ph, i, slot):
                        choose_on_vector(nc, g, name, k)

        iterations(dve, emit)
        for name in ("f2.rs", "f2.out", "l2a", "l2b"):
            side(name, Image(B - 1))


def expert_part(nc, ctx, g):
    (out_pairs, logits_dram, t2_pairs, ident_f, gates, pooled, expert_step) = (
        g[k] for k in ("out_pairs", "logits_dram", "t2_pairs", "ident_f", "gates", "pooled", "expert_step"))
    QUADS = E // 4
    BANKS = QUADS * HID // HALF

    def sb(name, shape, dt=F32):
        return ctx.enter_context(nc.sbuf_tensor(name, shape, dt))

    def ps(name, shape):
        return ctx.enter_context(nc.psum_tensor(name, shape, F32))

    def sem(name):
        return ctx.enter_context(nc.semaphore(name))

    w1_sb = sb("w1_sb", [C + 1, E, HID])
    w2_sb = sb("w2_sb", [P, E, 2, C])
    b2_sb = sb("b2_sb", [C, E])
    hidden = sb("hidden", [P, BANKS, HALF])
    hidden_t = sb("hidden_t", [P, QUADS, 2, P])
    gathered = sb("gathered", [C, NG, BG, E])
    by_image = sb("by_image", [P, NG, BG, C])
    total = sb("total", [P, NG, BG, NJ, 2, C])

    hidden_ps = ps("hidden_ps", [P, BANKS, HALF])
    turn = ps("turn", [P, 2, HALF])
    small_ps = ps("small_ps", [P, HALF])

    (w1_loaded, w2_loaded, b2_loaded, hidden_ready, gelu_done, units_turned, units_copied, out_ready, out_biased,
     image_turned, image_copied, diagonal_zero, sum_ready, sum_taken, out_stored) = [sem(n) for n in (
        "w1_loaded", "w2_loaded", "b2_loaded", "hidden_ready", "gelu_done", "units_turned", "units_copied", "out_ready",
        "out_biased", "image_turned", "image_copied", "diagonal_zero", "sum_ready", "sum_taken", "out_stored")]
    t2_loaded = [sem(f"t2_loaded{k}") for k in range(NG)]
    block = ctx.enter_context(nc.Block())
    SUMS = NJ
    STORES = sorted({SUMS // 2, NG * SUMS - SUMS // 2} | {SUMS * k for k in range(NG + 1)})
    LAST_GROUP = NG - 1

    @block.sync
    def _(sp):
        k = LAST_GROUP
        sp.dma_start(g["lg"][:, k % 2, :], logits_dram[k * BG:(k + 1) * BG].rearrange("b e s -> (b e) s")).then_inc(
            g["logits_loaded"][k], 16)
        sp.dma_start(w1_sb[:, :, :], g["w1"].rearrange("e d h -> d e h")).then_inc(w1_loaded, 16)
        for half in range(2):
            sp.dma_start(w2_sb[:, :, half, :], g["w2"][:, half * P:(half + 1) * P, :].rearrange("e h o -> h e o")).then_inc(
                w2_loaded, 16)
        sp.dma_start(b2_sb[:, :], g["b2_t"]).then_inc(b2_loaded, 16)
        for k in range(NG):
            for b in range(BG):
                sp.dma_start(total[:, k, b, :, :, :].rearrange("p j a c -> p j (a c)"), t2_pairs[k * BG + b]).then_inc(
                    t2_loaded[k], 16)
        for start, end in zip(STORES, STORES[1:]):
            k, r = divmod(start, SUMS)
            pairs = slice(r, r + end - start)
            sp.wait_ge(sum_taken, end)
            for b in range(BG):
                sp.dma_start(out_pairs[k * BG + b][:, pairs, :],
                             total[:, k, b, pairs, :, :].rearrange("p j a c -> p j (a c)")).then_inc(out_stored, 16)
        sp.wait_ge(out_stored, 16 * BG * (len(STORES) - 1))

    @block.tensor
    def _(pe):
        for name in EXPERT_STEPS:
            choose_on_tensor(nc, g, name, LAST_GROUP, turn[:, 0, :], small_ps[:, :])
        pe.wait_ge(w1_loaded, 16)
        pe.wait_ge(expert_step, done("expert_step", "e.turn", LAST_GROUP, "copy"))
        for quad in range(QUADS):
            bank, at = divmod(quad * HID, HALF)
            for r in range(4):
                mm = pe.matmul(hidden_ps[r * 32:(r + 1) * 32, bank, at:at + HID], pooled[:, quad * 4 + r, :],
                               w1_sb[:, quad * 4 + r, :], start=True, stop=True)
            if at + HID == HALF:
                mm.then_inc(hidden_ready, 1)
        for bank in range(BANKS):
            pe.wait_ge(gelu_done, bank + 1)
            if bank >= 2:
                pe.wait_ge(units_copied, bank - 1)
            for k in range(4):
                mm = pe.transpose(turn[:, bank % 2, k * P:(k + 1) * P], hidden[:, bank, k * P:(k + 1) * P], ident_f[:, :])
            mm.then_inc(units_turned, 1)
        pe.wait_ge(w2_loaded, 32)
        for bank in range(BANKS):
            pe.wait_ge(units_copied, bank + 1)
            for e in range(bank * E // BANKS, (bank + 1) * E // BANKS, 2):
                for half in range(2):
                    for odd in range(2):
                        quad, r = divmod(e + odd, 4)
                        mm = pe.matmul(small_ps[odd * C:(odd + 1) * C, e // 2 * B:(e // 2 + 1) * B],
                                       w2_sb[:, e + odd, half, :], hidden_t[:, quad, half, r * 32:r * 32 + B],
                                       start=half == 0, stop=half == 1, skip_group_check=True)
        mm.then_inc(out_ready, 1)
        pe.wait_ge(out_biased, 1)
        for k in range(NG):
            mm = pe.transpose(turn[:, 0, k * C:(k + 1) * C],
                              gathered[:, k, :, :].rearrange("c b e -> c (b e)"), ident_f[0:C, 0:C])
        mm.then_inc(image_turned, 1)
        pe.wait_ge(image_copied, 2)
        for k in range(NG):
            for r in range(SUMS):
                n = k * SUMS + r
                if n >= BANKS:
                    pe.wait_ge(sum_taken, n - BANKS + 1)
                for a in range(2):
                    mm = pe.matmul(hidden_ps[:, n % BANKS, a * BG * C:(a + 1) * BG * C],
                                   gates[:, k, 2 * r * P:2 * (r + 1) * P].rearrange("g (p a) -> g a p", a=2)[:, a, :],
                                   by_image[:, k, :, :].rearrange("p b c -> p (b c)"), start=True, stop=True)
                mm.then_inc(sum_ready, 1)

    def to_diagonal(copy, images):
        for b in images:
            r = slice(b * E, (b + 1) * E)
            ins = copy(by_image[r, :, b, :], turn[r, 0, 0:NG * C].rearrange("p (k c) -> p k c", c=C))
        ins.then_inc(image_copied, 1)

    @block.scalar
    def _(act):
        for name in EXPERT_STEPS:
            choose_on_scalar(nc, g, name, LAST_GROUP, turn[:, 0, :], small_ps[:, :])
        for bank in range(BANKS):
            act.wait_ge(hidden_ready, bank + 1)
            nc.scalar.activation(hidden[:, bank, :], hidden_ps[:, bank, :], ACT.Gelu).then_inc(gelu_done, 1)
        act.wait_ge(diagonal_zero, 1)
        act.wait_ge(image_turned, 1)
        to_diagonal(nc.scalar.copy, (2, 3))

    @block.vector
    def _(dve):
        V = nc.vector
        for name in EXPERT_STEPS:
            choose_on_vector(nc, g, name, LAST_GROUP)
        V.memset(by_image[:, :, :, :], 0.0).then_inc(diagonal_zero, 1)
        for bank in range(BANKS):
            dve.wait_ge(units_turned, bank + 1)
            per = QUADS // BANKS
            V.tensor_copy(hidden_t[:, bank * per:(bank + 1) * per, :, :].rearrange("p q h m -> p (q h m)"),
                          turn[:, bank % 2, :]).then_inc(units_copied, 1)
        dve.wait_ge(b2_loaded, 16)
        dve.wait_ge(out_ready, 1)
        for odd in range(2):
            ins = V.tensor_tensor(gathered[:, :, :, :].rearrange("c k b e -> c e (k b)")[:, odd::2, :],
                                  small_ps[odd * C:(odd + 1) * C, 0:E // 2 * B].rearrange("c (e b) -> c e b", b=B),
                                  b2_sb[:, odd::2].unsqueeze(2).to_broadcast([C, E // 2, B]), ALU.add)
        ins.then_inc(out_biased, 1)
        dve.wait_ge(diagonal_zero, 1)
        dve.wait_ge(image_turned, 1)
        to_diagonal(V.tensor_copy, (0, 1))
        for k in range(NG):
            dve.wait_ge(t2_loaded[k], 16 * BG)
            for r in range(SUMS):
                n = k * SUMS + r
                dve.wait_ge(sum_ready, n + 1)
                pairs = total[:, k, :, r, :, :].rearrange("p b a c -> p a b c")
                V.tensor_tensor(pairs, hidden_ps[:, n % BANKS, :].rearrange("p (a b c) -> p a b c", a=2, b=BG),
                                pairs, ALU.add).then_inc(sum_taken, 1)


def kernel(x, L0_conv_gn_scale, L0_conv_gn_bias, L0_conv_wq, L0_conv_bq, L0_conv_wk, L0_conv_bk, L0_conv_wv,
           L0_conv_bv, L0_conv_wo, L0_conv_bo, L1_attn_Wq, L1_attn_Wk, L1_attn_Wv, L1_ffn_gate_w, L1_ffn_gate_b,
           L1_ffn_weight1, L1_ffn_weight2):
    import concourse.bacc as bacc
    from concourse.bass_utils import run_bass_kernel_spmd

    asnp = lambda a: np.ascontiguousarray(np.asarray(a))
    column = lambda a: asnp(a).reshape(-1, 1)
    p = np.arange(P)
    same = (p[:, None] % C) // GROUP == (p[None, :] % C) // GROUP
    group_mean = (same / (2.0 * GROUP)).astype(np.float32)
    ident = np.eye(P, dtype=np.float32)
    causal_q = np.where(p[None, :] > p[:, None], MASKED, 0.0).astype(np.float32)
    block_rows = (np.arange(S)[None, :] // P == np.arange(NT)[:, None]).astype(np.float32)
    by_channel = {
        "wq": L0_conv_wq, "wk": L0_conv_wk, "wv_t": np.asarray(L0_conv_wv).T, "wo": L0_conv_wo,
        "a_wq": L1_attn_Wq, "a_wk": L1_attn_Wk, "a_wv_t": np.asarray(L1_attn_Wv).T,
        "gate_t": np.asarray(L1_ffn_gate_w).T, "gn_scale": column(L0_conv_gn_scale), "gn_bias": column(L0_conv_gn_bias),
        "bq": column(L0_conv_bq), "bk": column(L0_conv_bk), "bv": column(L0_conv_bv)}
    arrays = {
        "x": asnp(x).reshape(B, S, C),
        "by_channel": asnp(np.concatenate([np.asarray(by_channel[k]) for k in CHANNEL_CONSTS], axis=1)),
        "bo": asnp(L0_conv_bo).reshape(1, C), "gate_b": column(L1_ffn_gate_b),
        "w1": asnp(L1_ffn_weight1), "w2": asnp(L1_ffn_weight2),
        "b2_t": asnp(np.asarray(L1_ffn_weight2)[:, HID, :].T),
        "shape_masks": asnp(np.stack([group_mean, ident, causal_q, causal_q.T], axis=1)),
        "block_rows": block_rows,
    }
    nc = bacc.Bacc("TRN2", target_bir_lowering=False, num_devices=1)
    aps = {k: nc.dram_tensor(f"in_{k}", v.shape, mybir.dt.from_np(v.dtype), kind="ExternalInput").ap()
           for k, v in arrays.items()}
    out = nc.dram_tensor("out", (B, S, C), F32, kind="ExternalOutput").ap()
    build_program(nc, out=out, **aps)
    r = run_bass_kernel_spmd(nc, [{f"in_{k}": v for k, v in arrays.items()}], core_ids=[0])
    return r.results[0]["out"].reshape(B, 32, 32, C)
```
